# Optimizing a Trainium2 kernel written in Bass

```python
import numpy as np
import jax
import jax.numpy as jnp

def _softmax(x, axis=-1):
    return jax.nn.softmax(x, axis=axis)

def _gelu(x):
    return jax.nn.gelu(x, approximate=True)

def _silu(x):
    return jax.nn.silu(x)

def _sigmoid(x):
    return jax.nn.sigmoid(x)

def _layernorm(x, axis=-1, eps=1e-05):
    m = jnp.mean(x, axis=axis, keepdims=True)
    v = jnp.var(x, axis=axis, keepdims=True)
    return (x - m) / jnp.sqrt(v + eps)

def _scatter_add(tgt, idx, src, axis=0):
    return tgt.at[idx].add(src)

def _segment_sum(src, seg, n):
    return jax.ops.segment_sum(src, seg, n)
kernel_name = 'mk_decoder_postln_d1_seqx_r8_f85116'

def setup_inputs(seed: int=0):
    np.random.seed(seed)
    _w = jnp.asarray

    def _rec_inputs():
        import jax
        import jax.numpy as jnp
        _rk = jax.random.key(seed)
        x = 7.22e-05 + 1 * jax.random.normal(jax.random.fold_in(_rk, 1), (16, 128, 128), jnp.float32)
        _lenS = 128 - jax.random.randint(jax.random.fold_in(_rk, 7), (16,), 0, max(1, 128 // 4) + 1, jnp.int32)
        _lenS2 = 120 - jax.random.randint(jax.random.fold_in(_rk, 8), (16,), 0, max(1, 120 // 4) + 1, jnp.int32)
        _ctx_1024P = jax.random.normal(jax.random.fold_in(_rk, 11), (16, 16, 128), jnp.float32)
        _ctx_1024c = jax.random.dirichlet(jax.random.fold_in(_rk, 511), 0.3 * jnp.ones((16,), jnp.float32), (16, 120))
        _ctx_1024t = jnp.einsum('bsk,bkd->bsd', _ctx_1024c, _ctx_1024P)
        _ctx_1024t = _ctx_1024t * jax.lax.rsqrt(jnp.mean(jnp.square(_ctx_1024t)) + 1e-12) * 0.953939
        ctx_1024 = -0.000514642 + 1.00011 * (_ctx_1024t + 0.3 * jax.random.normal(jax.random.fold_in(_rk, 611), (16, 120, 128), jnp.float32))
        return (x, ctx_1024)
    x, ctx_1024 = _rec_inputs()

    def _L0_attn_setup():
        import jax, jax.numpy as jnp
        import numpy as np
        D_MODEL = 128
        NUM_HEADS = 16
        HEAD_DIM = D_MODEL // NUM_HEADS
        BATCH = 4
        SEQ = 256

        def circulant(x, c, b):
            d = c.shape[0]
            y = jnp.fft.irfft(jnp.fft.rfft(x, axis=-1) * jnp.fft.rfft(c), n=d, axis=-1)
            return y + b
        key = jax.random.key(seed)
        ks = jax.random.split(key, 9)
        scale = 1.0 / np.sqrt(D_MODEL)
        inp = {'x': jax.random.normal(ks[0], (BATCH, SEQ, D_MODEL), dtype=jnp.float32), 'wq_c': jax.random.normal(ks[1], (D_MODEL,), dtype=jnp.float32) * scale, 'wq_b': jnp.zeros((D_MODEL,), dtype=jnp.float32), 'wk_c': jax.random.normal(ks[2], (D_MODEL,), dtype=jnp.float32) * scale, 'wk_b': jnp.zeros((D_MODEL,), dtype=jnp.float32), 'wv_c': jax.random.normal(ks[3], (D_MODEL,), dtype=jnp.float32) * scale, 'wv_b': jnp.zeros((D_MODEL,), dtype=jnp.float32), 'wo_c': jax.random.normal(ks[4], (D_MODEL,), dtype=jnp.float32) * scale, 'wo_b': jnp.zeros((D_MODEL,), dtype=jnp.float32)}
        return inp
    _L0_attn_all = _L0_attn_setup()
    _L0_attn_in = {k: v for k, v in _L0_attn_all.items() if k in ('wq_c', 'wq_b', 'wk_c', 'wk_b', 'wv_c', 'wv_b', 'wo_c', 'wo_b')}
    del _L0_attn_all

    def _L0_xattn_setup():
        import jax, jax.numpy as jnp
        import numpy as np
        B, L_ENC, L_DEC, D = (16, 64, 128, 128)
        key = jax.random.key(seed)
        k1, k2, k3, k4, k5, k6 = jax.random.split(key, 6)
        encoder_hc = jax.random.normal(k1, (B, L_ENC, D), dtype=jnp.float32)
        decoder_hq = jax.random.normal(k2, (B, L_DEC, D), dtype=jnp.float32)
        w_sim = jax.random.normal(k3, (3 * D,), dtype=jnp.float32) * 0.02
        b_sim = jax.random.normal(k4, (1,), dtype=jnp.float32) * 0.02
        W_qv = jax.random.normal(k5, (4 * D, D), dtype=jnp.float32) * 0.02
        b_qv = jax.random.normal(k6, (D,), dtype=jnp.float32) * 0.02
        return {'encoder_hc': encoder_hc, 'decoder_hq': decoder_hq, 'w_sim': w_sim, 'b_sim': b_sim, 'W_qv': W_qv, 'b_qv': b_qv}
    _L0_xattn_all = _L0_xattn_setup()
    _L0_xattn_in = {k: v for k, v in _L0_xattn_all.items() if k in ('w_sim', 'b_sim', 'W_qv', 'b_qv')}
    del _L0_xattn_all

    def _L0_ffn_setup():
        import jax, jax.numpy as jnp
        import numpy as np
        ALPHA = 1.702
        LIMIT = 7.0
        TOPK = 2
        D, I, E = (128, 256, 8)
        B, S = (2, 256)

        def swiglu(x):
            g = x[..., ::2]
            l = x[..., 1::2]
            g = jnp.minimum(g, LIMIT)
            l = jnp.clip(l, -LIMIT, LIMIT)
            return g * jax.nn.sigmoid(ALPHA * g) * (l + 1.0)
        key = jax.random.key(seed)
        ks = jax.random.split(key, 16)
        sc = 0.02
        n = lambda k, shape, s=sc: jax.random.normal(k, shape, dtype=jnp.float32) * s
        return {'x': jax.random.normal(ks[0], (B, S, D), dtype=jnp.float32), 'gate_w': n(ks[1], (E, D)), 'gate_b': n(ks[2], (E,)), 'w1': n(ks[3], (E, D, 2 * I)), 'b1': n(ks[4], (E, 2 * I)), 'w3': n(ks[5], (E, D, 2 * I)), 'b3': n(ks[6], (E, 2 * I)), 'w2': n(ks[7], (E, I, D)), 'b2': n(ks[8], (E, D)), 'sw1': n(ks[9], (D, 2 * I)), 'sb1': n(ks[10], (2 * I,)), 'sw3': n(ks[11], (D, 2 * I)), 'sb3': n(ks[12], (2 * I,)), 'sw2': n(ks[13], (I, D)), 'sb2': n(ks[14], (D,))}
    _L0_ffn_all = _L0_ffn_setup()
    _L0_ffn_in = {k: v for k, v in _L0_ffn_all.items() if k in ('gate_w', 'gate_b', 'w1', 'b1', 'w3', 'b3', 'w2', 'b2', 'sw1', 'sb1', 'sw3', 'sb3', 'sw2', 'sb2')}
    del _L0_ffn_all
    return {'x': x, 'ctx_1024': ctx_1024, 'L0_attn_wq_c': _L0_attn_in['wq_c'], 'L0_attn_wq_b': _L0_attn_in['wq_b'], 'L0_attn_wk_c': _L0_attn_in['wk_c'], 'L0_attn_wk_b': _L0_attn_in['wk_b'], 'L0_attn_wv_c': _L0_attn_in['wv_c'], 'L0_attn_wv_b': _L0_attn_in['wv_b'], 'L0_attn_wo_c': _L0_attn_in['wo_c'], 'L0_attn_wo_b': _L0_attn_in['wo_b'], 'L0_xattn_w_sim': _L0_xattn_in['w_sim'], 'L0_xattn_b_sim': _L0_xattn_in['b_sim'], 'L0_xattn_W_qv': _L0_xattn_in['W_qv'], 'L0_xattn_b_qv': _L0_xattn_in['b_qv'], 'L0_ffn_gate_w': _L0_ffn_in['gate_w'], 'L0_ffn_gate_b': _L0_ffn_in['gate_b'], 'L0_ffn_w1': _L0_ffn_in['w1'], 'L0_ffn_b1': _L0_ffn_in['b1'], 'L0_ffn_w3': _L0_ffn_in['w3'], 'L0_ffn_b3': _L0_ffn_in['b3'], 'L0_ffn_w2': _L0_ffn_in['w2'], 'L0_ffn_b2': _L0_ffn_in['b2'], 'L0_ffn_sw1': _L0_ffn_in['sw1'], 'L0_ffn_sb1': _L0_ffn_in['sb1'], 'L0_ffn_sw3': _L0_ffn_in['sw3'], 'L0_ffn_sb3': _L0_ffn_in['sb3'], 'L0_ffn_sw2': _L0_ffn_in['sw2'], 'L0_ffn_sb2': _L0_ffn_in['sb2']}

def reference(x, ctx_1024, L0_attn_wq_c, L0_attn_wq_b, L0_attn_wk_c, L0_attn_wk_b, L0_attn_wv_c, L0_attn_wv_b, L0_attn_wo_c, L0_attn_wo_b, L0_xattn_w_sim, L0_xattn_b_sim, L0_xattn_W_qv, L0_xattn_b_qv, L0_ffn_gate_w, L0_ffn_gate_b, L0_ffn_w1, L0_ffn_b1, L0_ffn_w3, L0_ffn_b3, L0_ffn_w2, L0_ffn_b2, L0_ffn_sw1, L0_ffn_sb1, L0_ffn_sw3, L0_ffn_sb3, L0_ffn_sw2, L0_ffn_sb2):
    import jax
    import jax.numpy as jnp

    def _L0_attn_ref(x, wq_c, wq_b, wk_c, wk_b, wv_c, wv_b, wo_c, wo_b):
        import jax, jax.numpy as jnp
        import numpy as np
        D_MODEL = 128
        NUM_HEADS = 16
        HEAD_DIM = D_MODEL // NUM_HEADS
        BATCH = 4
        SEQ = 256

        def circulant(x, c, b):
            d = c.shape[0]
            y = jnp.fft.irfft(jnp.fft.rfft(x, axis=-1) * jnp.fft.rfft(c), n=d, axis=-1)
            return y + b
        bs, seq_len, dm = x.shape
        Q = circulant(x, wq_c, wq_b)
        K = circulant(x, wk_c, wk_b)
        V = circulant(x, wv_c, wv_b)
        Q = Q.reshape(bs, seq_len, NUM_HEADS, HEAD_DIM)
        K = K.reshape(bs, seq_len, NUM_HEADS, HEAD_DIM)
        V = V.reshape(bs, seq_len, NUM_HEADS, HEAD_DIM)
        scale = HEAD_DIM ** (-0.5)
        attn_logits = jnp.einsum('bqhd,bkhd->bhqk', Q, K) * scale
        attn_weights = jax.nn.softmax(attn_logits, axis=-1)
        out_heads = jnp.einsum('bhqk,bkhd->bqhd', attn_weights, V)
        out_merge = out_heads.reshape(bs, seq_len, dm)
        out = circulant(out_merge, wo_c, wo_b)
        return out

    def _L0_xattn_ref(encoder_hc, decoder_hq, w_sim, b_sim, W_qv, b_qv):
        import jax, jax.numpy as jnp
        import numpy as np
        B, L_ENC, L_DEC, D = (16, 64, 128, 128)
        d = encoder_hc.shape[-1]
        w1, w2, w3 = (w_sim[:d], w_sim[d:2 * d], w_sim[2 * d:])
        Sim = (encoder_hc @ w1)[:, :, None] + (decoder_hq @ w2)[:, None, :] + jnp.einsum('bid,bjd->bij', encoder_hc * w3, decoder_hq) + b_sim[0]
        A = jax.nn.softmax(Sim, axis=2)
        hq_hat = jnp.einsum('bij,bjd->bid', A, decoder_hq)
        Batt = jax.nn.softmax(jnp.max(Sim, axis=2), axis=1)
        hc_bar = jnp.einsum('bi,bid->bd', Batt, encoder_hc)[:, None, :]
        hc_hat = jnp.broadcast_to(hc_bar, encoder_hc.shape)
        feats = jnp.concatenate([encoder_hc, hq_hat, encoder_hc * hq_hat, encoder_hc * hc_hat], axis=-1)
        hcq = feats @ W_qv + b_qv
        return hcq

    def _L0_ffn_ref(x, gate_w, gate_b, w1, b1, w3, b3, w2, b2, sw1, sb1, sw3, sb3, sw2, sb2):
        import jax, jax.numpy as jnp
        import numpy as np
        ALPHA = 1.702
        LIMIT = 7.0
        TOPK = 2
        D, I, E = (128, 256, 8)
        B, S = (2, 256)

        def swiglu(x):
            g = x[..., ::2]
            l = x[..., 1::2]
            g = jnp.minimum(g, LIMIT)
            l = jnp.clip(l, -LIMIT, LIMIT)
            return g * jax.nn.sigmoid(ALPHA * g) * (l + 1.0)
        b, s, d = x.shape
        xt = x.reshape(-1, d)
        scores = jax.nn.softmax(xt @ gate_w.T, axis=-1)
        biased = scores + gate_b
        _, idx = jax.lax.top_k(biased, TOPK)
        weights = jnp.take_along_axis(scores, idx, axis=-1)
        comb = (weights[..., None] * jax.nn.one_hot(idx, E, dtype=xt.dtype)).sum(1)

        def body(acc, p):
            ew1, eb1, ew3, eb3, ew2, eb2, ce = p
            h = swiglu((xt @ ew1 + eb1) * (xt @ ew3 + eb3))
            return (acc + ce[:, None] * (h @ ew2 + eb2), None)
        routed, _ = jax.lax.scan(body, jnp.zeros_like(xt), (w1, b1, w3, b3, w2, b2, comb.T))
        shared = swiglu((xt @ sw1 + sb1) * (xt @ sw3 + sb3)) @ sw2 + sb2
        return (routed + shared).reshape(b, s, d)
    x = _layernorm(x + _L0_attn_ref(x, L0_attn_wq_c, L0_attn_wq_b, L0_attn_wk_c, L0_attn_wk_b, L0_attn_wv_c, L0_attn_wv_b, L0_attn_wo_c, L0_attn_wo_b), axis=-1)
    x = _layernorm(x + _L0_xattn_ref(x, ctx_1024, L0_xattn_w_sim, L0_xattn_b_sim, L0_xattn_W_qv, L0_xattn_b_qv), axis=-1)
    x = _layernorm(x + _L0_ffn_ref(x, L0_ffn_gate_w, L0_ffn_gate_b, L0_ffn_w1, L0_ffn_b1, L0_ffn_w3, L0_ffn_b3, L0_ffn_w2, L0_ffn_b2, L0_ffn_sw1, L0_ffn_sb1, L0_ffn_sw3, L0_ffn_sb3, L0_ffn_sw2, L0_ffn_sb2), axis=-1)
    return x

_drawn_inputs = setup_inputs


def setup_inputs(seed=0):
    import zlib

    import numpy as np

    out = dict(_drawn_inputs(seed))
    spreads = {'L0_attn_wq_b': (0.0, 0.527),
     'L0_attn_wk_b': (0.0, 2.0),
     'L0_attn_wv_b': (0.0, 0.1),
     'L0_attn_wo_b': (0.0, 0.1)}
    factors = {'L0_ffn_gate_w': 8.0,
     'L0_ffn_gate_b': 8.0,
     'L0_ffn_w1': 8.0,
     'L0_ffn_b1': 8.0,
     'L0_ffn_w3': 8.0,
     'L0_ffn_b3': 8.0,
     'L0_ffn_w2': 8.0,
     'L0_ffn_b2': 61.405,
     'L0_ffn_sw1': 6.867,
     'L0_ffn_sb1': 8.0,
     'L0_ffn_sw3': 6.936,
     'L0_ffn_sb3': 8.0,
     'L0_ffn_sw2': 6.859,
     'L0_ffn_sb2': 22.896}
    for name, (base, spread) in spreads.items():
        noise = np.random.default_rng([zlib.crc32(name.encode()), seed]).standard_normal(out[name].shape)
        drawn = base * np.exp(spread * noise) if base else spread * noise
        out[name] = jnp.asarray(drawn.astype(out[name].dtype))
    for name, factor in factors.items():
        out[name] = (out[name] * factor).astype(out[name].dtype)
    return out
```

```python
from contextlib import ExitStack

import numpy as np
import concourse.bass as bass
from concourse import mybir

F32 = mybir.dt.float32
F32R = mybir.dt.float32r
BF16 = mybir.dt.bfloat16
I32 = mybir.dt.int32
ALU = mybir.AluOpType
ACT = mybir.ActivationFunctionType
AX = mybir.AxisListType

P = 128
B = 16
D = 128
NC = 120
H, HD = 16, 8
E = 8
I2, I = 512, 256
G4 = 4
NG = B // G4
U = 4
HG = H // U
RQ = 3 * HD
RM = RQ + 2
SCALE = float(HD) ** -0.5
EPS = 1e-5
ALPHA, LIMIT = 1.702, 7.0
BIG = 1e30
NA = 12
NR = (2 * B * P + E * (P - 1)) // P
NT = NR + B
BROWS = ((E + 1) * I2 // P, (E + 1) * I2 // P, (E + 1) * D // P)
LEAD = 6
GROUP_STEPS = {-4: 0, -3: 1, 0: 2}
FIRST_SLOT, LAST_SLOT = -G4 * U - 4, 72
PREP_SLOT = -11
LOOP = NA + 4
ROUTE = 7
PAIRS = (NR - 5) // 2
FINAL = NA + NR + 4
SMALL = 12
LOGITS = 512 - B // 2 * E
FFN_SLOT = 66


def decoder_layer(nc, x, ctx_1024, wq_c, wq_b, wk_c, wk_b, wv_c, wv_b, wo_c, wo_b, w_sim, b_sim, W_qv, b_qv,
                  gate_w, gate_b, w1, b1, w3, b3, w2, b2, sw1, sb1, sw3, sb3, sw2, sb2, out):
    circ_scr = nc.dram_tensor("circ_scr", (4, P, 2 * D), F32)
    bias_scr = nc.dram_tensor("bias_scr", (3, sum(BROWS), P), BF16)
    parts_scr = nc.dram_tensor("parts_scr", (NG, 2, H, 3, HD, G4 * P), F32)
    xs = nc.dram_tensor("xs", (NR * P, D), F32)
    ys = nc.dram_tensor("ys", (NR * P, D), F32)

    ctx = ExitStack()
    with ctx:
        def sb(name, shape, dt=F32):
            return ctx.enter_context(nc.sbuf_tensor(name, shape, dt))

        def ps(name, shape):
            return ctx.enter_context(nc.psum_tensor(name, shape, F32))

        def sem(name):
            return ctx.enter_context(nc.semaphore(name))

        ident = sb("ident", [P, P])
        before = sb("before", [P, P])
        ones = sb("ones", [P, P])
        zeros = sb("zeros", [P, D])
        bias_rows = sb("bias_rows", [9, 3, P], BF16)
        head_ones = sb("head_ones", [P, U, 32])
        neg_half = sb("neg_half", [P, 1])
        iota8 = sb("iota8", [P, E])
        iota_t = sb("iota_t", [1, NR])
        circ = sb("circ", [P, 4, D])
        qk_bias = sb("qk_bias", [P, 2])
        bv_row = sb("bv_row", [P, D])
        bo_row = sb("bo_row", [P, D])
        bqv_row = sb("bqv_row", [P, D])
        gateb_row = sb("gateb_row", [P, E])
        ctx_sb = sb("ctx_sb", [NC, B, D])
        wqv = sb("wqv", [P, 4, D])
        wsim = sb("wsim", [P, 3])
        bsim = sb("bsim", [P, 1])
        gw_sb = sb("gw_sb", [E, D])
        gwT = sb("gwT", [P, E])
        sim_rhs = sb("sim_rhs", [P, B, NC])
        sim_row = sb("sim_row", [P, 4 * NC])
        ctxT = sb("ctxT", [P, 4 * NC])
        W1 = sb("W1", [P, (E + 1) * I2])
        W3 = sb("W3", [P, (E + 1) * I2])
        W2 = sb("W2", [P, (E + 1) * I])
        bias_f = sb("bias_f", [sum(BROWS), P])
        bparts = sb("bparts", [sum(BROWS), 3, P], BF16)
        bias3 = sb("bias3", [9, (E + 1) * I2], BF16)

        X = sb("X", [P, B, D])
        X2 = sb("X2", [P, B, D])
        X2T = sb("X2T", [P, 2, P])
        XT = sb("XT", [P, 2, G4 * P])
        qk_hi = sb("qk_hi", [P, 2, G4 * P], F32R)
        qk_lo = sb("qk_lo", [P, 2, G4 * P], F32R)
        Qst = sb("Qst", [P, 2, U, 2 * P], F32R)
        Kst = sb("Kst", [P, 2, U, 2 * P], F32R)
        Qdiag = sb("Qdiag", [P, 2, U, HG, P], F32R)
        Kdiag = sb("Kdiag", [P, 2, U, HG, P], F32R)
        Vz = sb("Vz", [P, 2, HG, U, 32])
        PT = sb("PT", [P, 4, HG * P])
        negmax = sb("negmax", [P, 2, H])
        max_parts = sb("max_parts", [P, 2, H], F32R)
        ident_r = sb("ident_r", [P, P], F32R)
        maxT = sb("maxT", [2 * H, 2, P])
        inv_den = sb("inv_den", [P, 2, P])
        attnT = sb("attnT", [P, 2, P])
        XB = sb("XB", [P, 2, D])

        R = sb("R", [P, 2, D])
        stats = sb("stats", [P, 2, 6])
        meanvar = sb("meanvar", [P, 2, 2])
        vareps = sb("vareps", [P, 2])
        rstd = sb("rstd", [P, 2])
        R2 = sb("R2", [P, 2, D])
        stats2 = sb("stats2", [P, 2, 6])
        meanvar2 = sb("meanvar2", [P, 2, 2])
        vareps2 = sb("vareps2", [P, 2])
        rstd2 = sb("rstd2", [P, 2])
        X1 = sb("X1", [P, 2, D])
        X1T = sb("X1T", [P, 2, P])
        X1B = sb("X1B", [P, 2, D])
        neg_rowmax = sb("neg_rowmax", [P, 2])
        Aexp = sb("Aexp", [P, 2, NC])
        Asum = sb("Asum", [P, 2])
        Ainv = sb("Ainv", [P, 2])
        A = sb("A", [P, 2, NC])
        AT = sb("AT", [NC, 2, P])
        top = sb("top", [1, 2])
        batt = sb("batt", [1, 2, P])
        batt_sum = sb("batt_sum", [1, 2])
        batt_inv = sb("batt_inv", [1, 2])
        batt_col = sb("batt_col", [P, 2])
        hqT = sb("hqT", [P, 2, P])
        hq_x = sb("hq_x", [P, 2, P])
        hc = sb("hc", [P, 2])
        wx = sb("wx", [P, 2, D])

        r3 = [P, B, E]
        logit = sb("logit", r3)
        rexp = sb("rexp", r3)
        score = sb("score", r3)
        biased = sb("biased", r3)
        rtmp = sb("rtmp", r3)
        cand = sb("cand", r3)
        pick = [sb("pick0", r3), sb("pick1", r3)]
        rtop = sb("rtop", [P, B])
        rsum = sb("rsum", [P, B])
        rinv = sb("rinv", [P, B])
        weight = sb("weight", [P, 2, B])
        count = sb("count", [P, E, B])
        before_tile = sb("before_tile", [P, E, B])
        total = sb("total", [P, E])
        tiles = sb("tiles", [P, E])
        tiles_cum = sb("tiles_cum", [P, E])
        row_base = sb("row_base", [P, E])
        slot_f = sb("slot_f", [P, 2, B])
        slot = sb("slot", [P, 2, B], I32)
        past = sb("past", [1, NR, E])
        tab_f = sb("tab_f", [1, NR])
        expert_of = sb("expert_of", [1, NT], I32)

        XR = sb("XR", [P, 2, D])
        XH = sb("XH", [P, 2, 3 * P])
        up1, prod = PT[:, 0:2, :], PT[:, 2:4, :]
        gclip, lclip = XT[:, 0, :].rearrange("p (q n) -> p q n", q=2), XT[:, 1, :].rearrange("p (q n) -> p q n", q=2)
        after_v = Vz[:].rearrange("p b g j c -> p (b g j c)")
        th, gate = (after_v[:, k * 2 * I:(k + 1) * 2 * I].rearrange("p (q n) -> p q n", q=2) for k in range(2))
        hid = sb("hid", [P, 2, I])
        YO = sb("YO", [P, 2, D])

        Z, Y1, Y2, R3, R4, R5, OUT = X, hqT, hq_x, R, X1, R2, wx
        stats3 = sb("stats3", [P, 2, 6])
        meanvar3 = sb("meanvar3", [P, 2, 2])
        vareps3 = sb("vareps3", [P, 2])
        rstd3 = sb("rstd3", [P, 2])

        pS = ps("pS", [P, 2, 512])
        pT = ps("pT", [P, 2, 512])
        pO = ps("pO", [P, 512])
        pM = ps("pM", [P, 512])
        pX = ps("pX", [P, 2, 512])

        s_x = [sem(f"s_x{g}") for g in range(NG)]
        s_circw = sem("s_circw")
        s_circ = sem("s_circ")
        s_small = sem("s_small")
        s_ctx = sem("s_ctx")
        s_biasf = sem("s_biasf")
        s_biasw = sem("s_biasw")
        s_bias3 = sem("s_bias3")
        s_w = [sem(f"s_w{e}") for e in range(E + 1)]
        s_parts = [[sem(f"s_parts{i}{g}") for g in range(NG)] for i in range(2)]
        s_stack = [sem("s_stack0"), sem("s_stack1")]
        s_kdiag = [sem("s_kdiag0"), sem("s_kdiag1")]
        s_qdiag = [sem("s_qdiag0"), sem("s_qdiag1")]
        s_maxrow = [sem("s_maxrow0"), sem("s_maxrow1")]
        s_xs_zero = sem("s_xs_zero")
        s_scat = sem("s_scat")
        s_load = [sem("s_load0"), sem("s_load1")]
        s_store = [sem("s_store0"), sem("s_store1")]
        s_y12 = [sem("s_y120"), sem("s_y121")]
        s_out = [sem("s_out0"), sem("s_out1")]
        c_pool = sem("c_pool")
        c_ident = sem("c_ident")
        c_zero = sem("c_zero")
        c_kdiag = sem("c_kdiag")
        c_v = sem("c_v")
        c_identr = sem("c_identr")
        c_bias = sem("c_bias")
        xT_ps, xT_sb = sem("xT_ps"), sem("xT_sb")
        qk_ps, hi_sb, lo_sb = sem("qk_ps"), sem("hi_sb"), sem("lo_sb")
        v_ps, v_sb = sem("v_ps"), sem("v_sb")
        xb_sb = sem("xb_sb")
        s_ps, max_sb = sem("s_ps"), sem("max_sb")
        mx_hi, mx_parts = sem("mx_hi"), sem("mx_parts")
        mxT_ps, mxT_sb = sem("mxT_ps"), sem("mxT_sb")
        sT_ps, p_sb, pv_ps = sem("sT_ps"), sem("p_sb"), sem("pv_ps")
        inv_sb, attn_sb = sem("inv_sb"), sem("attn_sb")
        o_ps, r_sb, st_sb, mv_sb, ve_sb, rs_sb, x1_sb = (sem(n) for n in ("o_ps", "r_sb", "st_sb", "mv_sb", "ve_sb", "rs_sb", "x1_sb"))
        x1T_ps, x1T_sb, x1b_sb = sem("x1T_ps"), sem("x1T_sb"), sem("x1b_sb")
        sim_ps, nm_sb, ae_sb, ai_sb, a_sb = (sem(n) for n in ("sim_ps", "nm_sb", "ae_sb", "ai_sb", "a_sb"))
        aT_ps, top_sb, be_sb, bi_sb, aT_sb = (sem(n) for n in ("aT_ps", "top_sb", "be_sb", "bi_sb", "aT_sb"))
        hq_ps, hq_sb, hqx_sb = sem("hq_ps"), sem("hq_sb"), sem("hqx_sb")
        hc_ps, hc_sb, wx_sb = sem("hc_ps"), sem("hc_sb"), sem("wx_sb")
        x2_ps, r2_sb, st2_sb, mv2_sb, ve2_sb, rs2_sb, x2_sb = (sem(n) for n in ("x2_ps", "r2_sb", "st2_sb", "mv2_sb", "ve2_sb", "rs2_sb", "x2_sb"))
        x2T_ps, x2T_sb = sem("x2T_ps"), sem("x2T_sb")
        gwT_ps, gwT_sb = sem("gwT_ps"), sem("gwT_sb")
        cT_ps, cT_sb, sr_sb, row_ps, row_sb = (sem(n) for n in ("cT_ps", "cT_sb", "sr_sb", "row_ps", "row_sb"))
        bias_step = sem("bias_step")
        w2_half = sem("w2_half")
        lg_ps, rt, rexp_sb, cnt_ps, slots_sb, tab_sb, picked = (
            sem(n) for n in ("lg_ps", "rt", "rexp_sb", "cnt_ps", "slots_sb", "tab_sb", "picked"))
        t_ps, xh_sb, a_ps, b_ps, up1_sb, prod_sb = (sem(n) for n in ("t_ps", "xh_sb", "a_ps", "b_ps", "up1_sb", "prod_sb"))
        g_sb, l_sb, th_sb, gt_sb, h_sb, y_ps, y_sb = (sem(n) for n in ("g_sb", "l_sb", "th_sb", "gt_sb", "h_sb", "y_ps", "y_sb"))
        f1_sb, f2_sb, f3_sb, fs_sb, fm_sb, fv_sb, fr_sb, fo_sb = (sem(n) for n in ("f1_sb", "f2_sb", "f3_sb", "fs_sb", "fm_sb", "fv_sb", "fr_sb", "fo_sb"))

        block = ctx.enter_context(nc.Block())

        def chain_steps(n):
            t, j = n // U, n % U
            found = [(t - 3, 8)] if j == 0 else []
            found.append((t - 2, 4 + j))
            if j:
                found.append((t - 1, j))
            return [(b, k) for b, k in found if 0 <= b < B]

        def group_step(n):
            for g in range(NG):
                if n - G4 * U * (g - 1) in GROUP_STEPS:
                    return g, GROUP_STEPS[n - G4 * U * (g - 1)]
            return None

        def shared_batch(pos):
            return pos if pos < NA else pos - NR

        def qcols(b):
            return slice((b % G4) * P, (b % G4 + 1) * P)

        @block.sync
        def _(sp):
            for g in range(1):
                sp.dma_start(X[:, 0:G4, :], x[0:G4].rearrange("b s d -> s b d")).then_inc(s_x[0], 16)
            for k, c in enumerate((wq_c, wk_c, wv_c, wo_c)):
                sp.dma_start(circ_scr.ap()[k].rearrange("p (r n) -> p r n", r=2),
                             bass.AP(c.tensor, 0, [[0, P], [0, 2], [1, D]])).then_inc(s_circw, 16)
            sp.wait_ge(s_circw, 64)
            for k in range(4):
                sp.dma_start(circ[:, k, :], bass.AP(circ_scr, k * P * 2 * D + D, [[2 * D - 1, P], [1, D]])).then_inc(s_circ, 16)
            small = [(qk_bias[:, 0:1], wq_b.rearrange("(p o) -> p o", o=1)), (qk_bias[:, 1:2], wk_b.rearrange("(p o) -> p o", o=1)),
                     (bv_row[:], bass.AP(wv_b.tensor, 0, [[0, P], [1, D]])), (bo_row[:], bass.AP(wo_b.tensor, 0, [[0, P], [1, D]])),
                     (bqv_row[:], bass.AP(b_qv.tensor, 0, [[0, P], [1, D]])), (gateb_row[:], bass.AP(gate_b.tensor, 0, [[0, P], [1, E]])),
                     (wqv[:], W_qv.rearrange("(k p) n -> p k n", p=P)), 
                     (bsim[:], bass.AP(b_sim.tensor, 0, [[0, P], [1, 1]])), (gw_sb[:], gate_w)]
            small += [(wsim[:, k:k + 1], w_sim[k * P:(k + 1) * P].rearrange("(p o) -> p o", o=1)) for k in range(3)]
            for to, src in small:
                sp.dma_start(to, src).then_inc(s_small, 16)
            sp.dma_start(ctx_sb[:], ctx_1024.rearrange("b j d -> j b d")).then_inc(s_ctx, 16)
            for g in range(1, NG):
                sp.dma_start(X[:, G4 * g:G4 * g + G4, :], x[G4 * g:G4 * g + G4].rearrange("b s d -> s b d")).then_inc(s_x[g], 16)

            def spill(g, i):
                sp.wait_ge(lo_sb, 2 * g + i + 1)
                for r, part in enumerate(((0, 0, 1), (0, 1, 0))[i]):
                    sp.dma_start(parts_scr.ap()[g, i, :, r], (qk_hi, qk_lo)[part][:, i, :].bitcast(F32)).then_inc(s_parts[i][g], 16)

            def parts_of(b, i, hg, batches=1):
                return parts_scr.ap()[b // G4, i, U * hg:U * (hg + 1), :, :, (b % G4) * P:(b % G4 + batches) * P].rearrange(
                    "h r d n -> (r d) h n")

            def stack(h):
                if h == 0:
                    sp.wait_ge(c_pool, 1)
                if h >= 2:
                    sp.wait_ge(sT_ps, 2 * U * (h - 1))
                for i, st in enumerate((Qst, Kst)):
                    sp.wait_ge(s_parts[i][h // 2], 48)
                    for hg in range(HG):
                        sp.dma_start(st[32 * hg:32 * hg + RQ, h % 2, :, :].bitcast(F32),
                                     parts_of(2 * h, i, hg, 2)).then_inc(s_stack[h % 2], 16)

            def k_diag(b):
                if b == 0:
                    sp.wait_ge(c_kdiag, 1)
                if b >= 2:
                    sp.wait_ge(s_ps, U * (b - 1))
                sp.wait_ge(s_parts[1][b // G4], 48)
                for hg in range(HG):
                    sp.dma_start(Kdiag[32 * hg:32 * hg + RQ, b % 2, :, hg, :].bitcast(F32),
                                 parts_of(b, 1, hg)).then_inc(s_kdiag[b % 2], 16)

            def q_diag(b):
                if b == 0:
                    sp.wait_ge(c_pool, 2)
                if b >= 2:
                    sp.wait_ge(sT_ps, U * (b - 1))
                sp.wait_ge(s_parts[0][b // G4], 48)
                for hg in range(HG):
                    sp.dma_start(Qdiag[32 * hg:32 * hg + RQ, b % 2, :, hg, :].bitcast(F32),
                                 parts_of(b, 0, hg)).then_inc(s_qdiag[b % 2], 16)

            def max_rows(b):
                sp.wait_ge(mxT_sb, b + 1)
                if b >= 2:
                    sp.wait_ge(sT_ps, U * (b - 1))
                for part in range(2):
                    sp.dma_start(Qdiag[RQ + part:RQ + part + 1, b % 2, :, :, :].rearrange("p j g n -> p (j g) n").bitcast(F32),
                                 maxT[H * part:H * (part + 1), b % 2, :]).then_inc(s_maxrow[b % 2], 16)

            def expert_weights(e):
                a, c, d = (w1[e], w3[e], w2[e]) if e < E else (sw1, sw3, sw2)
                sp.dma_start(W1[:, e * I2:(e + 1) * I2], a).then_inc(s_w[e], 16)
                sp.dma_start(W3[:, e * I2:(e + 1) * I2], c).then_inc(s_w[e], 16)
                sp.dma_start(W2[:, e * I:(e + 1) * I].rearrange("p (k n) -> p k n", k=2),
                             d.rearrange("(k p) n -> p k n", p=P)).then_inc(s_w[e], 16)

            def load(r, par):
                if not (isinstance(r, int) and r < 2):
                    sp.wait_ge(t_ps, NA - 1 + r)
                sp.dma_start(XR[:, par, :], xs.ap()[bass.ds(r * P, P), :]).then_inc(s_load[par], 16)

            def store(r, par):
                sp.wait_ge(y_sb, NA + r + 1)
                sp.dma_start(ys.ap()[bass.ds(r * P, P), :], YO[:, par, :]).then_inc(s_store[par], 16)

            for n in range(FIRST_SLOT, LAST_SLOT + 1):
                if n == PREP_SLOT:
                    row = 0
                    for routed, shared in ((b1, sb1), (b3, sb3), (b2, sb2)):
                        for src in (routed.rearrange("e (r p) -> (e r) p", p=P), shared.rearrange("(r p) -> r p", p=P)):
                            sp.dma_start(bias_f[row:row + src.shape[0], :], src).then_inc(s_biasf, 16)
                            row += src.shape[0]
                    sp.wait_ge(c_zero, 1)
                    sp.dma_start(xs.ap().rearrange("(t p) d -> p t d", p=P),
                                 bass.AP(zeros, 0, [[D, P], [0, NR], [1, D]])).then_inc(s_xs_zero, 16)
                for g in range(NG):
                    if n == G4 * U * (g - 1) - 2:
                        spill(g, 0)
                    if n == G4 * U * (g - 1) + 1:
                        spill(g, 1)
                if n % U == 2 and 0 <= (n + 10) // U < B:
                    k_diag((n + 10) // U)
                if n % (2 * U) == 0 and 0 <= n // (2 * U) + 1 < B // 2:
                    stack(n // (2 * U) + 1)
                if n % U == 0 and 0 <= n // U + 1 < B:
                    q_diag(n // U + 1)
                if n >= 0 and n % 3 == 1 and n // 3 <= E:
                    expert_weights(n // 3)
                if n == 30:
                    sp.wait_ge(bias_step, 5)
                    sp.dma_start(bias_scr.ap().rearrange("t r n -> r t n"), bparts[:]).then_inc(s_biasw, 16)
                if n == 34:
                    sp.wait_ge(s_biasw, 16)
                    sp.wait_ge(c_bias, 1)
                    row = 0
                    for k, rows in enumerate(BROWS):
                        sp.dma_start(bias3[3 * k:3 * k + 3, 0:rows * P],
                                     bias_scr.ap()[:, row:row + rows, :].rearrange("t r n -> t (r n)")).then_inc(s_bias3, 16)
                        row += rows
                if n >= -2 and n % U == 2 and (n + 2) // U < B:
                    max_rows((n + 2) // U)
            sp.wait_ge(s_scat, 16 * 2 * B)
            for i in range(5):
                load(i, i % 2)
            with sp.Fori(0, (NR - 5) // 2) as q:
                for u in range(2):
                    load(q * 2 + (5 + u), 1 - u)
                    store(q * 2 + u, u)
            for i in range(2 * ((NR - 5) // 2), NR):
                if i + 5 < NR:
                    load(i + 5, (i + 5) % 2)
                store(i, i % 2)
            for b in range(B):
                sp.wait_ge(fo_sb, b + 1)
                sp.dma_start(out[b], OUT[:, b % 2, :]).then_inc(s_out[b % 2], 16)
            for par in range(2):
                sp.wait_ge(s_out[par], 16 * B // 2)

        @block.gpsimd
        def _(pool):
            pool.memset(ident[:], 0.0).then_inc(c_ident, 1)
            pool.memset(ones[:], 1.0)
            pool.memset(zeros[:], 0.0).then_inc(c_zero, 1)
            pool.wait_ge(c_ident, 1)
            pool.affine_select(out=ident[:], in_=ident[:], compare_op=ALU.not_equal, fill=1.0, base=0,
                               pattern=[[-1, P]], channel_multiplier=1).then_inc(c_ident, 1)
            pool.memset(Kst[:].bitcast(F32), 1.0)
            pool.memset(Qst[:].bitcast(F32), 0.0).then_inc(c_pool, 1)
            pool.memset(Qdiag[:].bitcast(F32), 0.0).then_inc(c_pool, 1)
            pool.memset(head_ones[:], 0.0).then_inc(c_pool, 1)
            pool.memset(neg_half[:], -0.5)
            pool.memset(bias3[:], 0.0).then_inc(c_bias, 1)
            pool.memset(bias_rows[:], 1.0).then_inc(c_bias, 1)
            pool.wait_ge(c_bias, 2)
            pool.affine_select(out=bias_rows[:], in_=bias_rows[:], compare_op=ALU.is_ge, fill=0.0, base=0,
                               pattern=[[-3, 3], [0, P]], channel_multiplier=1).then_inc(c_bias, 1)
            pool.wait_ge(c_bias, 3)
            pool.affine_select(out=bias_rows[:], in_=bias_rows[:], compare_op=ALU.is_ge, fill=0.0, base=2,
                               pattern=[[3, 3], [0, P]], channel_multiplier=-1).then_inc(c_bias, 1)
            pool.wait_ge(c_pool, 3)
            for j in range(U):
                pool.memset(head_ones[:, j, HD * j:HD * (j + 1)], 1.0)
            pool.wait_ge(c_zero, 1)
            pool.affine_select(out=before[:], in_=ones[:], compare_op=ALU.is_gt, fill=0.0, base=0,
                               pattern=[[1, P]], channel_multiplier=-1)
            pool.iota(iota8[:], [[1, E]], base=-E, channel_multiplier=0, allow_small_or_imprecise_dtypes=True)
            pool.iota(iota_t[:], [[1, NR]], base=0, channel_multiplier=0, allow_small_or_imprecise_dtypes=True)
            pool.memset(expert_of[:], E).then_inc(c_pool, 1)

            def root(ag, ve, rs, mv, out_ve, out_rs, b):
                p = b % 2
                pool.wait_ge(ag, b + 1)
                pool.tensor_scalar(out_ve[:, p:p + 1], mv[:, p, 1:2], EPS, None, ALU.add).then_inc(ve, 1)
                pool.wait_ge(ve, b + 1)
                pool.tensor_tensor(out_rs[:, p:p + 1], out_ve[:, p:p + 1], neg_half[:], ALU.pow).then_inc(rs, 1)

            for n in range(FIRST_SLOT, LAST_SLOT + 1):
                if n % U == 0 and 0 <= n // U < B:
                    b = n // U
                    if b == 0:
                        pool.wait_ge(s_small, 16 * SMALL)
                    if b % G4 == 0:
                        pool.wait_ge(s_x[b // G4], 16)
                    if b >= 2:
                        pool.wait_ge(r_sb, b - 1)
                    pool.tensor_tensor(XB[:, b % 2, :], X[:, b, :], bo_row[:], ALU.add).then_inc(xb_sb, 1)
                if n >= 3 and n % 3 == 0 and n // 3 - 1 <= E:
                    e = n // 3 - 1
                    pool.wait_ge(s_w[e], 48)
                    pool.tensor_scalar(W2[:, e * I:(e + 1) * I], W2[:, e * I:(e + 1) * I], 0.5, None, ALU.mult).then_inc(w2_half, 1)
                if n == 0:
                    pool.wait_ge(s_biasf, 96)
                    pool.tensor_copy(bparts[:, 0, :], bias_f[:]).then_inc(bias_step, 1)
                    for part in (1, 2):
                        pool.wait_ge(bias_step, 2 * part - 1)
                        pool.tensor_tensor(bias_f[:], bias_f[:], bparts[:, part - 1, :], ALU.subtract).then_inc(bias_step, 1)
                        pool.wait_ge(bias_step, 2 * part)
                        pool.tensor_copy(bparts[:, part, :], bias_f[:]).then_inc(bias_step, 1)
                for b, k in chain_steps(n):
                    p = b % 2
                    if k == 1:
                        root(mv_sb, ve_sb, rs_sb, meanvar, vareps, rstd, b)
                    elif k == 2:
                        pool.wait_ge(x1_sb, b + 1)
                        pool.tensor_tensor(X1B[:, p, :], X1[:, p, :], bqv_row[:], ALU.add).then_inc(x1b_sb, 1)
                    elif k == 5:
                        pool.wait_ge(hq_sb, b + 1)
                        pool.tensor_tensor(hq_x[:, p, :], X1T[:, p, :], hqT[:, p, :], ALU.mult).then_inc(hqx_sb, 1)
                    elif k == 7:
                        root(mv2_sb, ve2_sb, rs2_sb, meanvar2, vareps2, rstd2, b)
            pool.wait_ge(slots_sb, 1)
            pool.wait_ge(s_xs_zero, 16)
            for b in range(B):
                for k in range(2):
                    pool.indirect_dma_start(xs.ap(), bass.IndirectOffsetOnAxis(ap=slot[:, k, b:b + 1], axis=0),
                                            X2[:, b, :], None).then_inc(s_scat, 16)
            for par in range(2):
                pool.wait_ge(s_store[par], 16 * ((NR - 1 - par) // 2 + 1))
            for b in range(B + 1):
                if b < B:
                    p = b % 2
                    if b >= 2:
                        pool.wait_ge(f3_sb, b - 1)
                    for k, Y in enumerate((Y1, Y2)):
                        pool.indirect_dma_start(Y[:, p, :], None, ys.ap(),
                                                bass.IndirectOffsetOnAxis(ap=slot[:, k, b:b + 1], axis=0)).then_inc(s_y12[p], 16)
                if b >= 1:
                    root(fm_sb, fv_sb, fr_sb, meanvar3, vareps3, rstd3, b - 1)

        @block.scalar
        def _(act):
            def context(q):
                act.wait_ge(cT_ps, q + 1)
                act.wait_ge(sr_sb, q + 1)
                act.copy(ctxT[:], pX[:, 1, 0:4 * NC]).then_inc(cT_sb, 1)
                act.wait_ge(row_ps, q + 1)
                act.activation(sim_row[32 * q:32 * q + 1, :], pX[32 * q:32 * q + 1, 0, 0:4 * NC], ACT.Identity,
                               bias=bsim[32 * q:32 * q + 1, :], scale=1.0).then_inc(row_sb, 1)

            def group(g, k):
                if k == 0:
                    act.wait_ge(xT_ps, g + 1)
                    if g >= 2:
                        act.wait_ge(v_ps, G4 * (g - 1))
                    act.copy(XT[:, g % 2, :], pM[:]).then_inc(xT_sb, 1)
                else:
                    i = k - 1
                    if g == 0 and k == 1:
                        act.wait_ge(s_small, 16 * SMALL)
                    act.wait_ge(qk_ps, 2 * g + i + 1)
                    if g:
                        act.wait_ge(s_parts[i][g - 1], 48)
                    act.activation(qk_hi[:, i, :], pM[:], ACT.Identity, bias=qk_bias[:, i:i + 1],
                                   scale=1.0).then_inc(hi_sb, 1)

            def exps(u):
                act.wait_ge(sT_ps, u + 1)
                if u >= 4:
                    act.wait_ge(pv_ps, u - 3)
                act.activation(PT[:, u % 4, :], pT[:, u % 2, :], ACT.Exp, scale=SCALE).then_inc(p_sb, 1)

            def chain(b, k):
                p = b % 2
                if k == 2:
                    act.wait_ge(x1T_ps, b + 1)
                    act.copy(X1T[:, p, :], pX[:, p, 0:P]).then_inc(x1T_sb, 1)
                elif k == 3:
                    act.wait_ge(nm_sb, b + 1)
                    act.activation(Aexp[:, p, :], pX[:, p, 0:NC], ACT.Exp, bias=neg_rowmax[:, p:p + 1], scale=1.0,
                                   accum_out=Asum[:, p:p + 1]).then_inc(ae_sb, 1)
                elif k == 4:
                    act.wait_ge(top_sb, b + 1)
                    act.activation(batt[:, p, :], pX[0:1, p, P:2 * P], ACT.Exp, bias=top[:, p:p + 1], scale=-1.0,
                                   accum_out=batt_sum[:, p:p + 1]).then_inc(be_sb, 1)
                    act.copy(AT[:, p, :], pX[0:NC, p, 0:P]).then_inc(aT_sb, 1)
                elif k == 5:
                    act.wait_ge(hq_ps, b + 1)
                    act.copy(batt_col[:, p:p + 1], pX[:, p, P:P + 1])
                    act.copy(hqT[:, p, :], pX[:, p, 0:P]).then_inc(hq_sb, 1)
                elif k == 6:
                    act.wait_ge(hc_ps, b + 1)
                    act.copy(hc[:, p:p + 1], pX[:, p, 0:1]).then_inc(hc_sb, 1)
                elif k == 8:
                    act.wait_ge(x2T_ps, b + 1)
                    act.copy(X2T[:, p, :], pX[:, p, 0:P]).then_inc(x2T_sb, 1)

            def front(n):
                early = [c for c in chain_steps(n) if c[1] >= 4]
                late = [c for c in chain_steps(n) if c[1] < 4]
                for b, k in early:
                    chain(b, k)
                if 0 <= n < U * B:
                    exps(n)
                for b, k in late:
                    chain(b, k)
                if n >= -2 and n % U == 2 and (n + 2) // U < B:
                    b = (n + 2) // U
                    act.wait_ge(mxT_ps, b + 1)
                    if b >= 2:
                        act.wait_ge(s_maxrow[b % 2], 2 * 16 * (b // 2))
                    act.copy(maxT[:, b % 2, :], pM[0:2 * H, 0:P]).then_inc(mxT_sb, 1)
                if group_step(n):
                    group(*group_step(n))

            def tile(m, p, stored, first=False, tanh=True, up=True, y=True):
                act.wait_ge(t_ps, m + 2)
                if first:
                    act.copy(XH[:, p, 2 * P:3 * P], pO[:, 2 * P:3 * P]).then_inc(xh_sb, 1)
                else:
                    act.copy(XH[:, p, :], pO[:, 0:3 * P]).then_inc(xh_sb, 1)
                if tanh:
                    act.wait_ge(g_sb, m)
                    act.activation(th[:, 1 - p, :], gclip[:, 1 - p, :], ACT.Tanh, scale=ALPHA / 2).then_inc(th_sb, 1)
                if up:
                    act.wait_ge(a_ps, m + 1)
                    act.copy(up1[:, p, :], pS[:, p, :]).then_inc(up1_sb, 1)
                if y:
                    act.wait_ge(y_ps, m - 1)
                    if stored is not None:
                        act.wait_ge(s_store[p], 16 * stored)
                    act.copy(YO[:, p, :] if y is True else y, pM[:, 0:D]).then_inc(y_sb, 1)

            def tile_static(m):
                routed = NA <= m - 2 < NA + NR
                tile(m, m % 2, (m - 2 - NA) // 2 if routed and m - 2 >= NA + 2 else None, first=m < 2, tanh=1 <= m <= NT,
                     up=0 <= m < NT, y=routed or (m >= 2 and Z[:, shared_batch(m - 2), :]))

            act.wait_ge(c_ident, 2)
            act.copy(ident_r[:], ident[:]).then_inc(c_identr, 1)
            for n in range(FIRST_SLOT, LAST_SLOT + 1):
                if n == PREP_SLOT:
                    act.wait_ge(gwT_ps, 1)
                    act.copy(gwT[:], pX[:, 0, 0:E]).then_inc(gwT_sb, 1)
                    for q in range(4):
                        context(q)
                front(n)
                if n >= FFN_SLOT - 1:
                    tile_static(n - FFN_SLOT)
            for m in range(LAST_SLOT - FFN_SLOT + 1, LOOP):
                tile_static(m)
                if m == ROUTE:
                    act.wait_ge(rt, 2)
                    act.activation(rexp[:], logit[:], ACT.Exp).then_inc(rexp_sb, 1)
            with act.Fori(0, PAIRS) as q:
                for u in range(2):
                    tile(q * 2 + (LOOP + u), u, q + 1)
            for m in range(LOOP + 2 * PAIRS, NT + 2):
                tile_static(m)

        @block.vector
        def _(dve):
            def context(q):
                dve.wait_ge(cT_ps, q + 1)
                dve.tensor_scalar(sim_rhs[:, 4 * q:4 * q + 4, :], pX[:, 1, 0:4 * NC].rearrange("p (b j) -> p b j", b=4),
                                  wsim[:, 2:3], wsim[:, 0:1], ALU.mult, ALU.add).then_inc(sr_sb, 1)

            def group(g, k):
                if k:
                    i = k - 1
                    dve.wait_ge(hi_sb, 2 * g + i + 1)
                    dve.scalar_tensor_tensor(out=qk_lo[:, i, :], in0=pM[:], scalar=qk_bias[:, i:i + 1],
                                             in1=qk_hi[:, i, :].bitcast(F32), op0=ALU.add, op1=ALU.subtract).then_inc(lo_sb, 1)

            def values(b):
                dve.wait_ge(v_ps, b + 1)
                if b == 0:
                    dve.wait_ge(c_v, 1)
                if b >= 2:
                    dve.wait_ge(pv_ps, U * (b - 1))
                to = bass.AP(Vz, (b % 2) * HG * U * 32, [[2 * HG * U * 32, P], [U * 32, HG], [32 + HD, U], [1, HD]])
                dve.tensor_tensor(to, pM[:, 0:D].rearrange("p (g j d) -> p g j d", g=HG, j=U),
                                  bv_row[:].rearrange("p (g j d) -> p g j d", g=HG, j=U), ALU.add).then_inc(v_sb, 1)

            def row_max(u):
                b, j = u // U, u % U
                dve.wait_ge(s_ps, u + 1)
                dve.tensor_reduce(out=negmax[:, b % 2, HG * j:HG * (j + 1)],
                                  in_=pS[:, u % 2, :].rearrange("p (g k) -> p g k", g=HG), axis=AX.X, op=ALU.max,
                                  negate=True).then_inc(max_sb, 1)
                if j == U - 1:
                    dve.wait_ge(max_sb, u + 1)
                    if b >= 1:
                        dve.wait_ge(mxT_ps, b)
                    dve.tensor_copy(max_parts[:, 0, :], negmax[:, b % 2, :]).then_inc(mx_hi, 1)
                    dve.wait_ge(mx_hi, b + 1)
                    dve.tensor_tensor(max_parts[:, 1, :], negmax[:, b % 2, :], max_parts[:, 0, :].bitcast(F32),
                                      ALU.subtract).then_inc(mx_parts, 1)

            def attention_out(b):
                p = b % 2
                dve.wait_ge(pv_ps, U * (b + 1))
                dve.reciprocal(inv_den[:, p, :], pO[:, P:2 * P]).then_inc(inv_sb, 1)
                dve.wait_ge(inv_sb, b + 1)
                dve.tensor_tensor(attnT[:, p, :], pO[:, 0:P], inv_den[:, p, :], ALU.mult).then_inc(attn_sb, 1)

            def norm_stats(b, src, st, mv, s_src, s_st, s_mv):
                p = b % 2
                dve.wait_ge(s_src, b + 1)
                dve.bn_stats(st[:, p, :], src[:, p, :]).then_inc(s_st, 1)
                dve.wait_ge(s_st, b + 1)
                dve.bn_aggr(mv[:, p, :], st[:, p, :]).then_inc(s_mv, 1)

            def chain_a(b, k):
                p = b % 2
                if k == 1:
                    dve.wait_ge(o_ps, b + 1)
                    dve.wait_ge(xb_sb, b + 1)
                    dve.tensor_tensor(R[:, p, :], pX[:, p, 0:D], XB[:, p, :], ALU.add).then_inc(r_sb, 1)
                    norm_stats(b, R, stats, meanvar, r_sb, st_sb, mv_sb)
                elif k == 3:
                    dve.wait_ge(sim_ps, b + 1)
                    dve.tensor_reduce(out=neg_rowmax[:, p:p + 1], in_=pX[:, p, 0:NC], axis=AX.X, op=ALU.max,
                                      negate=True).then_inc(nm_sb, 1)
                elif k == 4:
                    dve.wait_ge(aT_ps, b + 1)
                    dve.tensor_reduce(out=top[:, p:p + 1], in_=pX[0:1, p, P:2 * P], axis=AX.X, op=ALU.min).then_inc(top_sb, 1)
                elif k == 6:
                    dve.wait_ge(hc_sb, b + 1)
                    dve.scalar_tensor_tensor(out=wx[:, p, :], in0=wqv[:, 3, :], scalar=hc[:, p:p + 1], in1=wqv[:, 0, :],
                                             op0=ALU.mult, op1=ALU.add).then_inc(wx_sb, 1)
                elif k == 7:
                    dve.wait_ge(x2_ps, b + 1)
                    dve.wait_ge(x1b_sb, b + 1)
                    dve.tensor_tensor(R2[:, p, :], pX[:, p, 0:D], X1B[:, p, :], ALU.add).then_inc(r2_sb, 1)
                    norm_stats(b, R2, stats2, meanvar2, r2_sb, st2_sb, mv2_sb)

            def chain_b(b, k):
                p = b % 2
                if k == 1:
                    dve.wait_ge(rs_sb, b + 1)
                    dve.tensor_scalar(X1[:, p, :], R[:, p, :], meanvar[:, p, 0:1], rstd[:, p:p + 1], ALU.subtract,
                                      ALU.mult).then_inc(x1_sb, 1)
                elif k == 3:
                    dve.wait_ge(ae_sb, b + 1)
                    dve.reciprocal(Ainv[:, p:p + 1], Asum[:, p:p + 1]).then_inc(ai_sb, 1)
                    dve.wait_ge(ai_sb, b + 1)
                    dve.tensor_scalar(A[:, p, :], Aexp[:, p, :], Ainv[:, p:p + 1], None, ALU.mult).then_inc(a_sb, 1)
                elif k == 4:
                    dve.wait_ge(be_sb, b + 1)
                    dve.reciprocal(batt_inv[:, p:p + 1], batt_sum[:, p:p + 1]).then_inc(bi_sb, 1)
                elif k == 7:
                    dve.wait_ge(rs2_sb, b + 1)
                    dve.tensor_scalar(X2[:, b, :], R2[:, p, :], meanvar2[:, p, 0:1], rstd2[:, p:p + 1], ALU.subtract,
                                      ALU.mult).then_inc(x2_sb, 1)

            def front(n):
                steps = chain_steps(n)
                for b, k in steps:
                    if k >= 4:
                        chain_a(b, k)
                if 0 <= n + LEAD < U * B:
                    row_max(n + LEAD)
                for b, k in steps:
                    if k < 4:
                        chain_a(b, k)
                if group_step(n):
                    group(*group_step(n))
                if n % U == U - 1 and 0 <= (n + 1) // U < B:
                    values((n + 1) // U)
                if n % U == 0 and 1 <= n // U <= B:
                    attention_out(n // U - 1)
                for b, k in steps:
                    chain_b(b, k)

            def tile(i, p):
                dve.wait_ge(b_ps, i + 1)
                dve.wait_ge(up1_sb, i + 1)
                dve.tensor_tensor(prod[:, p, :], pT[:, p, :], up1[:, p, :], ALU.mult).then_inc(prod_sb, 1)
                dve.wait_ge(prod_sb, i + 1)
                dve.tensor_scalar(gclip[:, p, :], prod[:, p, 0:I2:2], LIMIT, None, ALU.min).then_inc(g_sb, 1)
                dve.tensor_scalar(lclip[:, p, :], prod[:, p, 1:I2:2], LIMIT, -LIMIT, ALU.min, ALU.max).then_inc(l_sb, 1)
                dve.wait_ge(th_sb, i + 1)
                dve.scalar_tensor_tensor(out=gate[:, p, :], in0=th[:, p, :], scalar=1.0, in1=gclip[:, p, :], op0=ALU.add,
                                         op1=ALU.mult).then_inc(gt_sb, 1)
                dve.wait_ge(l_sb, i + 1)
                dve.wait_ge(gt_sb, i + 1)
                dve.scalar_tensor_tensor(out=hid[:, p, :], in0=lclip[:, p, :], scalar=1.0, in1=gate[:, p, :], op0=ALU.add,
                                         op1=ALU.mult).then_inc(h_sb, 1)

            steps_done = [0]

            def link(ins):
                steps_done[0] += 1
                ins.then_inc(rt, 1)
                dve.wait_ge(rt, steps_done[0])

            def over_e(t):
                return t[:].rearrange("p (b o) -> p b o", o=1).to_broadcast([P, B, E])

            def of_e(t):
                return bass.AP(t, 0, [[E, P], [0, B], [1, E]])

            psum_logits = bass.AP(pX, LOGITS, [[2 * 512, P], [E, B // 2], [512, 2], [1, E]])
            psum_be = pX[:, 1, 0:B * E].rearrange("p (b e) -> p b e", b=B)

            def by_parity(t):
                return t.rearrange("p (c k) e -> p c k e", k=2)

            psum_cnt = pX[:, 1, B * E:2 * B * E].rearrange("p (b e) -> p e b", b=B)

            def route_softmax_top():
                dve.wait_ge(lg_ps, B)
                link(dve.tensor_reduce(out=rtop[:].rearrange("p (c k) -> p c k", k=2), in_=psum_logits, axis=AX.X, op=ALU.max))
                link(dve.tensor_tensor(by_parity(logit[:]), psum_logits, by_parity(over_e(rtop)), ALU.subtract))

            def choose(k, src):
                link(dve.tensor_reduce(out=rtop[:], in_=src[:], axis=AX.X, op=ALU.max))
                link(dve.tensor_tensor(cand[:], src[:], over_e(rtop), ALU.is_ge))
                link(dve.tensor_tensor(cand[:], cand[:], of_e(iota8), ALU.mult))
                link(dve.tensor_reduce(out=rtop[:], in_=cand[:], axis=AX.X, op=ALU.min))
                link(dve.tensor_tensor(pick[k][:], of_e(iota8), over_e(rtop), ALU.is_equal))

            def route_first():
                dve.wait_ge(rexp_sb, 1)
                link(dve.tensor_reduce(out=rsum[:], in_=rexp[:], axis=AX.X, op=ALU.add))
                link(dve.reciprocal(rinv[:], rsum[:]))
                link(dve.tensor_tensor(score[:], rexp[:], over_e(rinv), ALU.mult))
                dve.wait_ge(s_small, 16 * SMALL)
                link(dve.tensor_tensor(biased[:], score[:], of_e(gateb_row), ALU.add))
                choose(0, biased)

            def route_second():
                link(dve.scalar_tensor_tensor(out=rtmp[:], in0=pick[0][:], scalar=-BIG, in1=biased[:], op0=ALU.mult, op1=ALU.add))
                choose(1, rtmp)
                dve.tensor_tensor(biased[:], pick[0][:], pick[1][:], ALU.add).then_inc(picked, 1)
                for k in range(2):
                    link(dve.tensor_tensor(rtmp[:], pick[k][:], score[:], ALU.mult))
                    link(dve.tensor_reduce(out=weight[:, k, :], in_=rtmp[:], axis=AX.X, op=ALU.add))

            def route_slots():
                dve.wait_ge(cnt_ps, 1)
                link(dve.tensor_copy(count[:], psum_cnt))
                link(dve.tensor_tensor_scan(before_tile[:].rearrange("p e b -> p (e b)"), ones[:, 0:B * E],
                                            count[:].rearrange("p e b -> p (e b)"), 0.0, ALU.mult, ALU.add))
                link(dve.tensor_tensor(before_tile[:], before_tile[:], count[:], ALU.subtract))
                link(dve.tensor_reduce(out=total[:], in_=count[:], axis=AX.X, op=ALU.add))
                link(dve.tensor_scalar(tiles[:], total[:], 1.0 / P, (P - 1) / (2.0 * P), ALU.mult, ALU.add))
                link(dve.tensor_scalar(tiles[:], tiles[:], float(1 << 23), None, ALU.add))
                link(dve.tensor_scalar(tiles[:], tiles[:], float(1 << 23), None, ALU.subtract))
                link(dve.tensor_tensor_scan(tiles_cum[:], ones[:, 0:E], tiles[:], 0.0, ALU.mult, ALU.add))
                link(dve.tensor_tensor(row_base[:], tiles_cum[:], tiles[:], ALU.subtract))
                link(dve.tensor_scalar(row_base[:], row_base[:], float(P), None, ALU.mult))
                link(dve.tensor_tensor(row_base[:], row_base[:], before_tile[:, :, 0], ALU.subtract))
                link(dve.tensor_tensor(before_tile[:], before_tile[:],
                                       row_base[:].rearrange("p (e o) -> p e o", o=1).to_broadcast([P, E, B]), ALU.add))
                link(dve.tensor_tensor(cand[:], psum_be, before_tile[:].rearrange("p e b -> p b e"), ALU.add))
                for k in range(2):
                    link(dve.tensor_tensor(rtmp[:], pick[k][:], cand[:], ALU.mult))
                    link(dve.tensor_reduce(out=slot_f[:, k, :], in_=rtmp[:], axis=AX.X, op=ALU.add))
                dve.tensor_copy(slot[:], slot_f[:]).then_inc(slots_sb, 1)
                link(dve.tensor_tensor(past[:], iota_t[:].rearrange("p (t o) -> p t o", o=1).to_broadcast([1, NR, E]),
                                       bass.AP(tiles_cum, 0, [[E, 1], [0, NR], [1, E]]), ALU.is_ge))
                link(dve.tensor_reduce(out=tab_f[:], in_=past[:], axis=AX.X, op=ALU.add))
                dve.wait_ge(c_pool, 4)
                dve.tensor_scalar(expert_of[:, NA:NA + NR], tab_f[:], float(E - 1), None, ALU.min).then_inc(tab_sb, 1)

            routing = {ROUTE: route_softmax_top, ROUTE + 1: route_first, ROUTE + 2: route_second, ROUTE + 3: route_slots}

            def final_a(b):
                p = b % 2
                dve.wait_ge(y_sb, (b if b < NA else NR + b) + 1)
                dve.tensor_tensor(R3[:, p, :], X2[:, b, :], Z[:, b, :], ALU.add).then_inc(f1_sb, 1)
                dve.wait_ge(s_y12[p], 32 * (b // 2 + 1))
                dve.wait_ge(f1_sb, b + 1)
                dve.scalar_tensor_tensor(out=R4[:, p, :], in0=Y1[:, p, :], scalar=weight[:, 0, b:b + 1], in1=R3[:, p, :],
                                         op0=ALU.mult, op1=ALU.add).then_inc(f2_sb, 1)
                dve.wait_ge(f2_sb, b + 1)
                dve.scalar_tensor_tensor(out=R5[:, p, :], in0=Y2[:, p, :], scalar=weight[:, 1, b:b + 1], in1=R4[:, p, :],
                                         op0=ALU.mult, op1=ALU.add).then_inc(f3_sb, 1)
                norm_stats(b, R5, stats3, meanvar3, f3_sb, fs_sb, fm_sb)

            def final_b(b):
                p = b % 2
                dve.wait_ge(fr_sb, b + 1)
                if b >= 2:
                    dve.wait_ge(s_out[p], 16 * (b // 2))
                dve.tensor_scalar(OUT[:, p, :], R5[:, p, :], meanvar3[:, p, 0:1], rstd3[:, p:p + 1], ALU.subtract,
                                  ALU.mult).then_inc(fo_sb, 1)

            def final(b):
                if b < B:
                    final_a(b)
                if b >= 1:
                    final_b(b - 1)

            dve.memset(Kdiag[:].bitcast(F32), 0.0).then_inc(c_kdiag, 1)
            dve.memset(Vz[:], 0.0).then_inc(c_v, 1)
            for n in range(FIRST_SLOT, LAST_SLOT + 1):
                if n == PREP_SLOT:
                    dve.wait_ge(s_small, 16 * SMALL)
                    for q in range(4):
                        context(q)
                front(n)
                if n >= FFN_SLOT + 1:
                    tile(n - FFN_SLOT - 1, (n - FFN_SLOT - 1) % 2)
            for m in range(LAST_SLOT - FFN_SLOT + 1, LOOP):
                tile(m - 1, (m - 1) % 2)
                if m in routing:
                    routing[m]()
            with dve.Fori(0, PAIRS) as q:
                for u in range(2):
                    tile(q * 2 + (LOOP - 1 + u), (LOOP - 1 + u) % 2)
            for m in range(LOOP + 2 * PAIRS, NT + 2):
                if m <= NT:
                    tile(m - 1, (m - 1) % 2)
                if m >= FINAL:
                    final(m - FINAL)
            for b in range(NT + 2 - FINAL, B + 1):
                final(b)

        @block.tensor
        def _(pe):
            issued = {"qk": 0, "v": 0, "x": 0, "m": 0}

            def projections_free():
                for s, k in ((xT_sb, "x"), (lo_sb, "qk"), (v_sb, "v"), (mxT_sb, "m")):
                    if issued[k]:
                        pe.wait_ge(s, issued[k])

            def group(g, k):
                projections_free()
                if k == 0:
                    pe.wait_ge(s_x[g], 16)
                    pe.wait_ge(c_ident, 2)
                    for c in range(G4):
                        mm = pe.transpose(pM[:, c * P:(c + 1) * P], X[:, g * G4 + c, :], ident[:])
                    mm.then_inc(xT_ps, 1)
                    issued["x"] += 1
                else:
                    pe.wait_ge(s_circ, 64)
                    pe.wait_ge(xT_sb, g + 1)
                    pe.matmul(pM[:], circ[:, k - 1, :], XT[:, g % 2, :], start=True, stop=True).then_inc(qk_ps, 1)
                    issued["qk"] += 1

            def values(b):
                projections_free()
                pe.matmul(pM[:, 0:D], XT[:, (b // G4) % 2, qcols(b)], circ[:, 2, :], start=True, stop=True).then_inc(v_ps, 1)
                issued["v"] += 1

            def scores(u):
                b, j = u // U, u % U
                pe.wait_ge(s_stack[(b // 2) % 2], 2 * HG * 16 * (b // 4 + 1))
                pe.wait_ge(s_kdiag[b % 2], HG * 16 * (b // 2 + 1))
                if u >= 2:
                    pe.wait_ge(max_sb, u - 1)
                pe.matmul(pS[:, u % 2, :], Qst[:, (b // 2) % 2, j, (b % 2) * P:(b % 2 + 1) * P],
                          Kdiag[:, b % 2, j, :, :], start=True, stop=True).then_inc(s_ps, 1)

            def scores_less_max(u):
                b, j = u // U, u % U
                pe.wait_ge(s_qdiag[b % 2], HG * 16 * (b // 2 + 1))
                pe.wait_ge(s_maxrow[b % 2], 2 * 16 * (b // 2 + 1))
                if u >= 2:
                    pe.wait_ge(p_sb, u - 1)
                pe.matmul(pT[:, u % 2, :], Kst[:, (b // 2) % 2, j, (b % 2) * P:(b % 2 + 1) * P],
                          Qdiag[:, b % 2, j, :, :], start=True, stop=True).then_inc(sT_ps, 1)

            def weighted_values(u):
                b, j = u // U, u % U
                pe.wait_ge(p_sb, u + 1)
                if u == 0:
                    pe.wait_ge(c_pool, 4)
                if j == 0:
                    pe.wait_ge(v_sb, b + 1)
                    if b >= 1:
                        pe.wait_ge(attn_sb, b)
                for hg in range(HG):
                    pe.matmul(pO[32 * hg:32 * hg + 32, 0:P], Vz[:, b % 2, hg, j, :], PT[:, u % 4, hg * P:(hg + 1) * P],
                              start=(j == 0), stop=(j == U - 1), skip_group_check=True)
                for hg in range(HG):
                    mm = pe.matmul(pO[32 * hg:32 * hg + 32, P:2 * P], head_ones[:, j, :], PT[:, u % 4, hg * P:(hg + 1) * P],
                                   start=False, stop=(j == U - 1), skip_group_check=True)
                mm.then_inc(pv_ps, 1)

            def max_transposes(b):
                projections_free()
                pe.wait_ge(mx_parts, b + 1)
                if b == 0:
                    pe.wait_ge(c_identr, 1)
                pe.matmul(pM[0:2 * H, 0:P], max_parts[:].rearrange("p k h -> p (k h)"), ident_r[:], start=True,
                          stop=True).then_inc(mxT_ps, 1)
                issued["m"] += 1

            def logits(b):
                pe.wait_ge(x2T_sb, b + 1)
                pe.matmul(pX[:, b % 2, LOGITS + b // 2 * E:LOGITS + (b // 2 + 1) * E], X2T[:, b % 2, :], gwT[:],
                          start=True, stop=True).then_inc(lg_ps, 1)

            def chain(b, k):
                p = b % 2
                if k == 1:
                    pe.wait_ge(attn_sb, b + 1)
                    if b >= 2:
                        logits(b - 2)
                    else:
                        pe.wait_ge(row_sb, 4)
                        pe.wait_ge(cT_sb, 4)
                    pe.matmul(pX[:, p, 0:D], attnT[:, p, :], circ[:, 3, :], start=True, stop=True).then_inc(o_ps, 1)
                elif k == 2:
                    pe.wait_ge(x1_sb, b + 1)
                    pe.transpose(pX[:, p, 0:P], X1[:, p, :], ident[:]).then_inc(x1T_ps, 1)
                elif k == 3:
                    pe.wait_ge(x1T_sb, b + 1)
                    pe.wait_ge(sr_sb, 4)
                    pe.matmul(pX[:, p, 0:NC], X1T[:, p, :], sim_rhs[:, b, :], start=True, stop=False)
                    q = 32 * (b // 4)
                    pe.matmul(pX[:, p, 0:NC], ones[q:q + 1, :], sim_row[q:q + 1, (b % 4) * NC:(b % 4 + 1) * NC], start=False,
                              stop=True).then_inc(sim_ps, 1)
                elif k == 4:
                    pe.wait_ge(a_sb, b + 1)
                    pe.transpose(pX[0:NC, p, 0:P], A[:, p, :], ident[:])
                    pe.matmul(pX[0:1, p, P:2 * P], neg_rowmax[:, p:p + 1], ident[:], start=True, stop=True).then_inc(aT_ps, 1)
                elif k == 5:
                    pe.wait_ge(aT_sb, b + 1)
                    pe.wait_ge(bi_sb, b + 1)
                    pe.wait_ge(s_ctx, 16)
                    pe.matmul(pX[:, p, 0:P], ctx_sb[:, b, :], AT[:, p, :], start=True, stop=True)
                    pe.matmul(pX[:, p, P:P + 1], batt[:, p, :], batt_inv[:, p:p + 1], start=True, stop=True).then_inc(hq_ps, 1)
                elif k == 6:
                    pe.wait_ge(hq_sb, b + 1)
                    pe.matmul(pX[:, p, 0:1], X1[:, p, :], batt_col[:, p:p + 1], start=True, stop=True).then_inc(hc_ps, 1)
                elif k == 7:
                    pe.wait_ge(wx_sb, b + 1)
                    pe.wait_ge(hqx_sb, b + 1)
                    pe.matmul(pX[:, p, 0:D], X1T[:, p, :], wx[:, p, :], start=True, stop=False)
                    pe.matmul(pX[:, p, 0:D], hqT[:, p, :], wqv[:, 1, :], start=False, stop=False)
                    pe.matmul(pX[:, p, 0:D], hq_x[:, p, :], wqv[:, 2, :], start=False, stop=True).then_inc(x2_ps, 1)
                elif k == 8:
                    pe.wait_ge(x2_sb, b + 1)
                    pe.transpose(pX[:, p, 0:P], X2[:, b, :], ident[:]).then_inc(x2T_ps, 1)

            def front(n):
                steps = chain_steps(n)
                if 0 <= n + LEAD < U * B:
                    scores(n + LEAD)
                for b, k in steps:
                    if k >= 4:
                        chain(b, k)
                if 0 <= n < U * B:
                    scores_less_max(n)
                for b, k in steps:
                    if k < 4:
                        chain(b, k)
                if 0 <= n - 1 < U * B:
                    weighted_values(n - 1)
                if n >= -2 and n % U == 2 and (n + 2) // U < B:
                    max_transposes((n + 2) // U)
                if group_step(n):
                    group(*group_step(n))
                if n % U == U - 1 and 0 <= (n + 1) // U < B:
                    values((n + 1) // U)

            def tile(m, p, rows, loaded, e_up, e_y, hidden=True, up=True, y=True):
                if loaded is not None:
                    pe.wait_ge(s_load[1 - p], 16 * loaded)
                if hidden:
                    pe.wait_ge(h_sb, m - 1)
                pe.wait_ge(xh_sb, m + 1) if not (isinstance(m, int) and m < 0) else None
                if hidden:
                    for k in range(2):
                        mm = pe.transpose(pO[:, k * P:(k + 1) * P], hid[:, p, k * P:(k + 1) * P], ident[:])
                if rows is not None:
                    mm = pe.transpose(pO[:, 2 * P:3 * P], rows, ident[:])
                mm.then_inc(t_ps, 1)

                def product(bank, W, k, done, free):
                    if not (isinstance(m, int) and m < 2):
                        pe.wait_ge(free, m - 1)
                    pe.matmul(bank, XH[:, 1 - p, 2 * P:3 * P], W[:, bass.ds(e_up * I2, I2)], start=True, stop=False)
                    pe.matmul(bank, bias_rows[:, k, :], bias3[:, bass.ds(e_up * I2, I2)], start=False,
                              stop=True).then_inc(done, 1)

                if up:
                    product(pS[:, p, :], W1, 0, a_ps, up1_sb)
                if y:
                    pe.wait_ge(xh_sb, m + 2)
                    if not (isinstance(m, int) and m < 3):
                        pe.wait_ge(y_sb, m - 2)
                    for k in range(2):
                        pe.matmul(pM[:, 0:D], XH[:, p, k * P:(k + 1) * P], W2[:, bass.ds(e_y * I + k * D, D)],
                                  start=(k == 0), stop=False)
                    pe.matmul(pM[:, 0:D], bias_rows[:, 2, :], bias3[:, bass.ds(e_y * D, D)], start=False,
                              stop=True).then_inc(y_ps, 1)
                if up:
                    product(pT[:, p, :], W3, 1, b_ps, prod_sb)

            def expert(i):
                return pe.value_load(expert_of[0:1, bass.ds(i, 1)], min_val=0, max_val=E)

            def tile_static(m, e_up=E, e_y=E):
                rows, loaded = None, None
                if NA <= m + 1 < NA + NR:
                    rows, loaded = XR[:, (m + 1) % 2, :], (m + 1 - NA) // 2 + 1
                elif m + 1 < NT:
                    rows = X2[:, shared_batch(m + 1), :]
                tile(m, m % 2, rows, loaded, e_up, e_y, hidden=m >= 2, up=0 <= m < NT, y=m >= 2)

            for n in range(FIRST_SLOT, LAST_SLOT + 1):
                if n == PREP_SLOT:
                    pe.wait_ge(s_small, 16 * SMALL)
                    pe.transpose(pX[:, 0, 0:E], gw_sb[:], ident[0:E, 0:E]).then_inc(gwT_ps, 1)
                    pe.wait_ge(s_ctx, 16)
                    for q in range(4):
                        if q:
                            pe.wait_ge(cT_sb, q)
                        for c in range(4):
                            mm = pe.transpose(pX[:, 1, c * NC:(c + 1) * NC], ctx_sb[:, 4 * q + c, :], ident[0:NC, 0:NC])
                        mm.then_inc(cT_ps, 1)
                        pe.wait_ge(cT_sb, q + 1)
                        if q:
                            pe.wait_ge(row_sb, q)
                        else:
                            pe.wait_ge(gwT_sb, 1)
                        pe.matmul(pX[32 * q:32 * q + 1, 0, 0:4 * NC], wsim[:, 1:2], ctxT[:], start=True, stop=True).then_inc(row_ps, 1)
                front(n)
                if n == FFN_SLOT - 1:
                    projections_free()
                    pe.wait_ge(attn_sb, B)
                    pe.wait_ge(max_sb, U * B)
                    pe.wait_ge(p_sb, U * B)
                    for e in range(E + 1):
                        pe.wait_ge(s_w[e], 48)
                    pe.wait_ge(w2_half, E + 1)
                    pe.wait_ge(s_bias3, 48)
                    pe.wait_ge(c_bias, 4)
                if n >= FFN_SLOT - 1:
                    tile_static(n - FFN_SLOT)
            logits(B - 2)
            logits(B - 1)
            for m in range(LAST_SLOT - FFN_SLOT + 1, LOOP):
                if m == ROUTE + 3:
                    pe.wait_ge(picked, 1)
                    both = biased[:].rearrange("p b e -> p (b e)")
                    pe.matmul(pX[:, 1, 0:B * E], before[:], both, start=True, stop=True)
                    pe.matmul(pX[:, 1, B * E:2 * B * E], ones[:], both, start=True, stop=True).then_inc(cnt_ps, 1)
                if m == NA:
                    pe.wait_ge(tab_sb, 1)
                tile_static(m, e_up=E if m < NA else expert(m), e_y=E if m - 2 < NA else expert(m - 2))
            with pe.Fori(0, PAIRS) as q:
                for u in range(2):
                    m = q * 2 + (LOOP + u)
                    tile(m, u, XR[:, 1 - u, :], q + (5 + u) // 2 + 1, expert(m), expert(m - 2))
            for m in range(LOOP + 2 * PAIRS, NT + 2):
                tile_static(m, e_up=E if m >= NA + NR or m >= NT else expert(m), e_y=E if m - 2 >= NA + NR else expert(m - 2))


_INS = ["x", "ctx_1024", "L0_attn_wq_c", "L0_attn_wq_b", "L0_attn_wk_c", "L0_attn_wk_b", "L0_attn_wv_c", "L0_attn_wv_b",
        "L0_attn_wo_c", "L0_attn_wo_b", "L0_xattn_w_sim", "L0_xattn_b_sim", "L0_xattn_W_qv", "L0_xattn_b_qv",
        "L0_ffn_gate_w", "L0_ffn_gate_b", "L0_ffn_w1", "L0_ffn_b1", "L0_ffn_w3", "L0_ffn_b3", "L0_ffn_w2", "L0_ffn_b2",
        "L0_ffn_sw1", "L0_ffn_sb1", "L0_ffn_sw3", "L0_ffn_sb3", "L0_ffn_sw2", "L0_ffn_sb2"]


def kernel(**inputs):
    import concourse.bacc as _bacc
    from concourse.bass_utils import run_bass_kernel_spmd as _run

    nc = _bacc.Bacc("TRN2", target_bir_lowering=False, num_devices=1)
    arrays, args = {}, []
    for name in _INS:
        a = np.ascontiguousarray(inputs[name])
        arrays[f"in_{name}"] = a
        args.append(nc.dram_tensor(f"in_{name}", a.shape, mybir.dt.from_np(a.dtype), kind="ExternalInput").ap())
    args.append(nc.dram_tensor("out_0", (B, P, D), F32, kind="ExternalOutput").ap())
    decoder_layer(nc, *args)
    r = _run(nc, [arrays], core_ids=[0])
    return r.results[0]["out_0"]
```

```python
from contextlib import ExitStack

import numpy as np
import concourse.bass as bass
from concourse import mybir

F32 = mybir.dt.float32
F32R = mybir.dt.float32r
BF16 = mybir.dt.bfloat16
I32 = mybir.dt.int32
ALU = mybir.AluOpType
ACT = mybir.ActivationFunctionType
AX = mybir.AxisListType

P = 128
B = 16
D = 128
NC = 120
H, HD = 16, 8
E = 8
I2, I = 512, 256
G4 = 4
NG = B // G4
U = 4
HG = H // U
RQ = 3 * HD
RM = RQ + 2
SCALE = float(HD) ** -0.5
EPS = 1e-5
ALPHA, LIMIT = 1.702, 7.0
BIG = 1e30
NA = 16
NR = (2 * B * P + E * (P - 1)) // P
NT = NR + B
BROWS = ((E + 1) * I2 // P, (E + 1) * I2 // P, (E + 1) * D // P)
LEAD = 6
GROUP_STEPS = {-4: 0, -3: 1, 0: 2}
FIRST_SLOT, LAST_SLOT = -G4 * U - 4, 72
EARLY = (7,)
MIDDLE = (5, 6)
PREP_SLOT = -11
LOOP = NA + 4
ROUTE = 7
PAIRS = (NR - 5) // 2
QUADS = (NR - 7) // 4
XW = D + 2
CAP = B * P + P
DUMMY = E * CAP
TOKENS = B * P
SMALL = 10
COUNT_STEP, ROUTE_STEPS = 7, 10
ROUTE_SLOT = 25
SCATTER_SLOT = ROUTE_SLOT + ROUTE_STEPS
FFN_SLOT = 67


def decoder_layer(nc, x, ctx_1024, wq_c, wq_b, wk_c, wk_b, wv_c, wv_b, wo_c, wo_b, w_sim, b_sim, W_qv, b_qv,
                  gate_w, gate_b, w1, b1, w3, b3, w2, b2, sw1, sb1, sw3, sb3, sw2, sb2, out):
    circ_scr = nc.dram_tensor("circ_scr", (4, P, 2 * D), F32)
    bias_scr = nc.dram_tensor("bias_scr", (3, sum(BROWS), P), BF16)
    parts_scr = nc.dram_tensor("parts_scr", (NG, 2, H, 3, HD, G4 * P), F32)
    xs = nc.dram_tensor("xs", (DUMMY + P, XW), F32)
    ys = nc.dram_tensor("ys", (2 * TOKENS + P, D), F32)

    ctx = ExitStack()
    with ctx:
        def sb(name, shape, dt=F32):
            return ctx.enter_context(nc.sbuf_tensor(name, shape, dt))

        def ps(name, shape):
            return ctx.enter_context(nc.psum_tensor(name, shape, F32))

        def sem(name):
            return ctx.enter_context(nc.semaphore(name))

        ident = sb("ident", [P, P])
        before = sb("before", [P, P])
        ones = sb("ones", [P, P])
        bias_rows = sb("bias_rows", [9, 3, P], BF16)
        head_ones = sb("head_ones", [P, U, 32])
        neg_half = sb("neg_half", [P, 1])
        iota8 = sb("iota8", [P, E])
        iota_t = sb("iota_t", [1, NR])
        iota_rows = sb("iota_rows", [1, NR])
        region = sb("region", [P, E])
        zero = sb("zero", [P, 1])
        dest = sb("dest", [P, 2, B])
        pad_row = sb("pad_row", [P, XW])
        circ = sb("circ", [P, 4, D])
        qk_bias = sb("qk_bias", [P, 2])
        bv_row = sb("bv_row", [P, D])
        bo_row = sb("bo_row", [P, D])
        bqv_row = sb("bqv_row", [P, D])
        gateb_row = sb("gateb_row", [P, E])
        ctx_sb = sb("ctx_sb", [NC, B, D])
        wqv = sb("wqv", [P, 4, D])
        wsim = sb("wsim", [P, 3])
        bsim = sb("bsim", [P, 1])
        gw_sb = sb("gw_sb", [E, D])
        gwT = sb("gwT", [P, E])
        sim_rhs = sb("sim_rhs", [P, B, NC])
        sim_row = sb("sim_row", [P, 4 * NC])
        ctxT = sb("ctxT", [P, 4 * NC])
        W1 = sb("W1", [P, (E + 1) * I2])
        W3 = sb("W3", [P, (E + 1) * I2])
        W2 = sb("W2", [P, (E + 1) * I])
        bias_f = sb("bias_f", [sum(BROWS), P])
        bparts = sb("bparts", [sum(BROWS), 3, P], BF16)
        bias3 = sb("bias3", [9, (E + 1) * I2], BF16)

        X = sb("X", [P, B, D])
        X2 = sb("X2", [P, B, XW])
        X2T = sb("X2T", [P, 2, P])
        XT = sb("XT", [P, 2, G4 * P])
        qk_hi = sb("qk_hi", [P, 2, G4 * P], F32R)
        qk_lo = sb("qk_lo", [P, 2, G4 * P], F32R)
        Qst = sb("Qst", [P, 2, U, 2 * P], F32R)
        Kst = sb("Kst", [P, 2, U, 2 * P], F32R)
        Qdiag = sb("Qdiag", [P, 2, U, HG, P], F32R)
        Kdiag = sb("Kdiag", [P, 2, U, HG, P], F32R)
        Vz = sb("Vz", [P, 2, HG, U, 32])
        PT = sb("PT", [P, 4, HG * P])
        negmax = sb("negmax", [P, 2, H])
        max_parts = sb("max_parts", [P, 2, H], F32R)
        ident_r = sb("ident_r", [P, P], F32R)
        maxT = sb("maxT", [2 * H, 2, P])
        inv_den = sb("inv_den", [P, 2, P])
        attnT = sb("attnT", [P, 2, P])
        XB = sb("XB", [P, 2, D])

        R = sb("R", [P, 2, D])
        stats = sb("stats", [P, 2, 6])
        meanvar = sb("meanvar", [P, 2, 2])
        vareps = sb("vareps", [P, 2])
        rstd = sb("rstd", [P, 2])
        R2 = sb("R2", [P, 2, D])
        stats2 = sb("stats2", [P, 2, 6])
        meanvar2 = sb("meanvar2", [P, 2, 2])
        vareps2 = sb("vareps2", [P, 2])
        rstd2 = sb("rstd2", [P, 2])
        X1 = sb("X1", [P, 2, D])
        X1T = sb("X1T", [P, 2, P])
        X1B = sb("X1B", [P, 2, D])
        neg_rowmax = sb("neg_rowmax", [P, 2])
        Aexp = sb("Aexp", [P, 2, NC])
        Asum = sb("Asum", [P, 2])
        Ainv = sb("Ainv", [P, 2])
        A = sb("A", [P, 2, NC])
        AT = sb("AT", [NC, 2, P])
        top = sb("top", [1, 2])
        batt = sb("batt", [1, 2, P])
        batt_sum = sb("batt_sum", [1, 2])
        batt_inv = sb("batt_inv", [1, 2])
        batt_col = sb("batt_col", [P, 2])
        hqT = sb("hqT", [P, 2, P])
        hq_x = sb("hq_x", [P, 2, P])
        hc = sb("hc", [P, 2])
        wx = sb("wx", [P, 2, D])

        logit = sb("logit", [P, B, E])
        rexp = sb("rexp", [P, G4, E])
        biased = sb("biased", [P, G4, E])
        cand = sb("cand", [P, G4, E])
        both = sb("both", [P, G4, E])
        pick = sb("pick", [P, 2, G4, E])
        picked_of = sb("picked_of", [P, 2, G4, E])
        rtop = sb("rtop", [P, G4])
        rinv = sb("rinv", [P, G4])
        weight_f = sb("weight_f", [P, 2, G4])
        weight = sb("weight", [P, 2, B])
        first_row = sb("first_row", [P, G4 + 1, E])
        total = sb("total", [P, E])
        tiles = sb("tiles", [P, E])
        tiles_cum = sb("tiles_cum", [P, E])
        start = sb("start", [P, E + 1])
        step = sb("step", [P, E])
        slot_f = sb("slot_f", [P, 2, G4])
        slot = sb("slot", [P, 2, B], I32)
        pad_start = sb("pad_start", [1, E], I32)
        past = sb("past", [1, NR, E])
        past_step = sb("past_step", [1, NR, E])
        tab_f = sb("tab_f", [1, NR])
        row_f = sb("row_f", [1, NR])
        expert_of = sb("expert_of", [1, NT], I32)
        row_of = sb("row_of", [1, NR], I32)

        XR = sb("XR", [P, 2, XW])
        row_dest = sb("row_dest", [P, 4], I32)
        row_weight = sb("row_weight", [P, 4])
        XH = sb("XH", [P, 2, 3 * P])
        up1, prod = PT[:, 0:2, :], PT[:, 2:4, :]
        gclip, lclip = XT[:, 0, :].rearrange("p (q n) -> p q n", q=2), XT[:, 1, :].rearrange("p (q n) -> p q n", q=2)
        after_v = Vz[:].rearrange("p b g j c -> p (b g j c)")
        th, gate = (after_v[:, k * 2 * I:(k + 1) * 2 * I].rearrange("p (q n) -> p q n", q=2) for k in range(2))
        hid = sb("hid", [P, 2, I])
        YO = sb("YO", [P, 2, D])

        Z = X
        Y = [t[:].bitcast(F32).rearrange("p k j (c n) -> p (k j c) n", n=D) for t in (Qst, Kst)]
        S = PT
        stats3 = sb("stats3", [P, B, 6])
        meanvar3 = sb("meanvar3", [P, B, 2])
        vareps3 = sb("vareps3", [P, B])
        rstd3 = sb("rstd3", [P, B])
        shift3 = sb("shift3", [P, B])

        pS = ps("pS", [P, 2, 512])
        pT = ps("pT", [P, 2, 512])
        pO = ps("pO", [P, 512])
        pM = ps("pM", [P, 512])
        pX = ps("pX", [P, 2, 512])

        s_x = [sem(f"s_x{g}") for g in range(NG)]
        s_circw = sem("s_circw")
        s_circ = sem("s_circ")
        s_small = sem("s_small")
        s_qkb = sem("s_qkb")
        s_ctx = sem("s_ctx")
        s_biasf = sem("s_biasf")
        s_biasw = sem("s_biasw")
        s_bias3 = sem("s_bias3")
        s_w = [sem(f"s_w{e}") for e in range(E + 1)]
        s_parts = [[sem(f"s_parts{i}{g}") for g in range(NG)] for i in range(2)]
        s_qst = [sem("s_qst0"), sem("s_qst1")]
        s_kst = [sem("s_kst0"), sem("s_kst1")]
        s_kdiag = [sem("s_kdiag0"), sem("s_kdiag1")]
        s_qdiag = [sem("s_qdiag0"), sem("s_qdiag1")]
        s_maxrow = [sem("s_maxrow0"), sem("s_maxrow1")]
        s_dummy = sem("s_dummy")
        s_scat, s_pad = sem("s_scat"), sem("s_pad")
        s_load = [sem("s_load0"), sem("s_load1")]
        s_ysc = [sem("s_ysc0"), sem("s_ysc1")]
        s_y = [sem(f"s_y{g}") for g in range(NG)]
        s_out = sem("s_out")
        c_pool = sem("c_pool")
        c_ident = sem("c_ident")
        c_zero = sem("c_zero")
        c_kdiag = sem("c_kdiag")
        c_v = sem("c_v")
        c_identr = sem("c_identr")
        c_bias = sem("c_bias")
        xT_ps, xT_sb = sem("xT_ps"), sem("xT_sb")
        qk_ps, hi_sb, lo_sb = sem("qk_ps"), sem("hi_sb"), sem("lo_sb")
        v_ps, v_sb = sem("v_ps"), sem("v_sb")
        xb_sb = sem("xb_sb")
        s_ps, max_sb = sem("s_ps"), sem("max_sb")
        mx_hi, mx_parts = sem("mx_hi"), sem("mx_parts")
        mxT_ps, mxT_sb = sem("mxT_ps"), sem("mxT_sb")
        sT_ps, p_sb, pv_ps = sem("sT_ps"), sem("p_sb"), sem("pv_ps")
        inv_sb, attn_sb = sem("inv_sb"), sem("attn_sb")
        o_ps, r_sb, st_sb, mv_sb, ve_sb, rs_sb, x1_sb = (sem(n) for n in ("o_ps", "r_sb", "st_sb", "mv_sb", "ve_sb", "rs_sb", "x1_sb"))
        x1T_ps, x1T_sb, x1b_sb = sem("x1T_ps"), sem("x1T_sb"), sem("x1b_sb")
        sim_ps, nm_sb, ae_sb, ai_sb, a_sb = (sem(n) for n in ("sim_ps", "nm_sb", "ae_sb", "ai_sb", "a_sb"))
        aT_ps, top_sb, be_sb, bi_sb, aT_sb = (sem(n) for n in ("aT_ps", "top_sb", "be_sb", "bi_sb", "aT_sb"))
        hq_ps, hq_sb, hqx_sb = sem("hq_ps"), sem("hq_sb"), sem("hqx_sb")
        hc_ps, hc_sb, wx_sb = sem("hc_ps"), sem("hc_sb"), sem("wx_sb")
        x2_ps, r2_sb, st2_sb, mv2_sb, ve2_sb, rs2_sb, x2_sb = (sem(n) for n in ("x2_ps", "r2_sb", "st2_sb", "mv2_sb", "ve2_sb", "rs2_sb", "x2_sb"))
        x2T_ps, x2T_sb = sem("x2T_ps"), sem("x2T_sb")
        gwT_ps, gwT_sb = sem("gwT_ps"), sem("gwT_sb")
        cT_ps, cT_sb, sr_sb, row_ps, row_sb = (sem(n) for n in ("cT_ps", "cT_sb", "sr_sb", "row_ps", "row_sb"))
        bias_step = sem("bias_step")
        w2_half = sem("w2_half")
        lg_ps, lg_sb, rt, rlog_sb, rexp_sb, picked, cnt_ps, cnt_sb, slots_sb, tab_sb, pad_sb, marked = (
            sem(n) for n in ("lg_ps", "lg_sb", "rt", "rlog_sb", "rexp_sb", "picked", "cnt_ps", "cnt_sb", "slots_sb", "tab_sb", "pad_sb", "marked"))
        t_ps, xh_sb, a_ps, b_ps, up1_sb, prod_sb = (sem(n) for n in ("t_ps", "xh_sb", "a_ps", "b_ps", "up1_sb", "prod_sb"))
        g_sb, l_sb, th_sb, gt_sb, h_sb, y_ps, y_sb = (sem(n) for n in ("g_sb", "l_sb", "th_sb", "gt_sb", "h_sb", "y_ps", "y_sb"))
        meta_sb = sem("meta_sb")
        f1_sb, f2_sb, f3_sb, fs_sb, fm_sb, fv_sb, fr_sb, fo_sb, fo2_sb = (
            sem(n) for n in ("f1_sb", "f2_sb", "f3_sb", "fs_sb", "fm_sb", "fv_sb", "fr_sb", "fo_sb", "fo2_sb"))

        block = ctx.enter_context(nc.Block())

        def chain_steps(n):
            t, j = n // U, n % U
            found = [(t - 2, 4 + j)] + ([(t - 3, 8)] if j == 0 else [])
            if j:
                found.append((t - 1, j))
            return [(b, k) for b, k in found if 0 <= b < B]

        def group_step(n):
            for g in range(NG):
                if n - G4 * U * (g - 1) in GROUP_STEPS:
                    return g, GROUP_STEPS[n - G4 * U * (g - 1)]
            return None

        def logit_bank(b):
            return pM[:, 0:E] if b < B - 2 else pX[:, b % 2, 0:E]

        def count_bank(g):
            return pM[:, 0:2 * G4 * E] if g < NG - 1 else pX[:, 1, 0:2 * G4 * E]

        def shared_batch(pos):
            return pos if pos < NA else pos - NR

        def qcols(b):
            return slice((b % G4) * P, (b % G4 + 1) * P)

        @block.sync
        def _(sp):
            sp.dma_start(X[:, 0:G4, :], x[0:G4].rearrange("b s d -> s b d")).then_inc(s_x[0], 16)
            for k, c in enumerate((wq_c, wk_c, wv_c, wo_c)):
                sp.dma_start(circ_scr.ap()[k].rearrange("p (r n) -> p r n", r=2),
                             bass.AP(c.tensor, 0, [[0, P], [0, 2], [1, D]])).then_inc(s_circw, 16)
            for i, src in enumerate((wq_b, wk_b)):
                sp.dma_start(qk_bias[:, i:i + 1], src.rearrange("(p o) -> p o", o=1)).then_inc(s_qkb, 16)
            sp.wait_ge(s_circw, 64)
            for k in range(4):
                sp.dma_start(circ[:, k, :], bass.AP(circ_scr, k * P * 2 * D + D, [[2 * D - 1, P], [1, D]])).then_inc(s_circ, 16)
            small = [(bv_row[:], bass.AP(wv_b.tensor, 0, [[0, P], [1, D]])), (bo_row[:], bass.AP(wo_b.tensor, 0, [[0, P], [1, D]])),
                     (bqv_row[:], bass.AP(b_qv.tensor, 0, [[0, P], [1, D]])), (gateb_row[:], bass.AP(gate_b.tensor, 0, [[0, P], [1, E]])),
                     (wqv[:], W_qv.rearrange("(k p) n -> p k n", p=P)),
                     (bsim[:], bass.AP(b_sim.tensor, 0, [[0, P], [1, 1]])), (gw_sb[:], gate_w)]
            small += [(wsim[:, k:k + 1], w_sim[k * P:(k + 1) * P].rearrange("(p o) -> p o", o=1)) for k in range(3)]
            for to, src in small:
                sp.dma_start(to, src).then_inc(s_small, 16)
            sp.dma_start(ctx_sb[:], ctx_1024.rearrange("b j d -> j b d")).then_inc(s_ctx, 16)
            for g in range(1, NG):
                sp.dma_start(X[:, G4 * g:G4 * g + G4, :], x[G4 * g:G4 * g + G4].rearrange("b s d -> s b d")).then_inc(s_x[g], 16)

            def spill(g, i):
                sp.wait_ge(lo_sb, 2 * g + i + 1)
                for r, part in enumerate(((0, 0, 1), (0, 1, 0))[i]):
                    sp.dma_start(parts_scr.ap()[g, i, :, r], (qk_hi, qk_lo)[part][:, i, :].bitcast(F32)).then_inc(s_parts[i][g], 16)

            def parts_of(b, i, hg, batches=1):
                return parts_scr.ap()[b // G4, i, U * hg:U * (hg + 1), :, :, (b % G4) * P:(b % G4 + batches) * P].rearrange(
                    "h r d n -> (r d) h n")

            def q_stack(h):
                if h == 0:
                    sp.wait_ge(c_pool, 1)
                if h >= 2:
                    sp.wait_ge(s_ps, 2 * U * (h - 1))
                sp.wait_ge(s_parts[0][h // 2], 48)
                for hg in range(HG):
                    sp.dma_start(Qst[32 * hg:32 * hg + RQ, h % 2, :, :].bitcast(F32),
                                 parts_of(2 * h, 0, hg, 2)).then_inc(s_qst[h % 2], 16)

            def k_stack(h):
                if h >= 2:
                    sp.wait_ge(sT_ps, 2 * U * (h - 1))
                sp.wait_ge(s_parts[1][h // 2], 48)
                for hg in range(HG):
                    sp.dma_start(Kst[32 * hg:32 * hg + RQ, h % 2, :, :].bitcast(F32),
                                 parts_of(2 * h, 1, hg, 2)).then_inc(s_kst[h % 2], 16)

            def k_diag(b):
                if b == 0:
                    sp.wait_ge(c_kdiag, 1)
                if b >= 2:
                    sp.wait_ge(s_ps, U * (b - 1))
                sp.wait_ge(s_parts[1][b // G4], 48)
                for hg in range(HG):
                    sp.dma_start(Kdiag[32 * hg:32 * hg + RQ, b % 2, :, hg, :].bitcast(F32),
                                 parts_of(b, 1, hg)).then_inc(s_kdiag[b % 2], 16)

            def q_diag(b):
                if b == 0:
                    sp.wait_ge(c_pool, 2)
                if b >= 2:
                    sp.wait_ge(sT_ps, U * (b - 1))
                sp.wait_ge(s_parts[0][b // G4], 48)
                for hg in range(HG):
                    sp.dma_start(Qdiag[32 * hg:32 * hg + RQ, b % 2, :, hg, :].bitcast(F32),
                                 parts_of(b, 0, hg)).then_inc(s_qdiag[b % 2], 16)

            def max_rows(b):
                sp.wait_ge(mxT_sb, b + 1)
                if b >= 2:
                    sp.wait_ge(sT_ps, U * (b - 1))
                for part in range(2):
                    sp.dma_start(Qdiag[RQ + part:RQ + part + 1, b % 2, :, :, :].rearrange("p j g n -> p (j g) n").bitcast(F32),
                                 maxT[H * part:H * (part + 1), b % 2, :]).then_inc(s_maxrow[b % 2], 16)

            def expert_weights(e):
                a, c, d = (w1[e], w3[e], w2[e]) if e < E else (sw1, sw3, sw2)
                sp.dma_start(W1[:, e * I2:(e + 1) * I2], a).then_inc(s_w[e], 16)
                sp.dma_start(W3[:, e * I2:(e + 1) * I2], c).then_inc(s_w[e], 16)
                sp.dma_start(W2[:, e * I:(e + 1) * I].rearrange("p (k n) -> p k n", k=2),
                             d.rearrange("(k p) n -> p k n", p=P)).then_inc(s_w[e], 16)

            def load(r, par):
                row = sp.value_load(row_of[0:1, bass.ds(r, 1)], min_val=0, max_val=DUMMY)
                if isinstance(r, int) and 2 <= r < 5:
                    sp.wait_ge(t_ps, NA - 1 + r)
                if not (isinstance(r, int) and r < 2):
                    sp.wait_ge(meta_sb, r - 1)
                sp.dma_start(XR[:, par, :], xs.ap()[bass.ds(row, P), :]).then_inc(s_load[par], 16)

            for n in range(FIRST_SLOT, LAST_SLOT + 1):
                for g in range(NG):
                    if n == G4 * U * (g - 1) - 2:
                        spill(g, 0)
                    if n == G4 * U * (g - 1) + 1:
                        spill(g, 1)
                if n >= -2 and n % U == 2 and (n + 2) // U < B:
                    max_rows((n + 2) // U)
                if n % U == 2 and 0 <= (n + 10) // U < B:
                    k_diag((n + 10) // U)
                if n % (2 * U) == 6 and 0 <= (n + 10) // (2 * U) < B // 2:
                    q_stack((n + 10) // (2 * U))
                if n % (2 * U) == 0 and 0 <= n // (2 * U) + 1 < B // 2:
                    k_stack(n // (2 * U) + 1)
                if n % U == 0 and 0 <= n // U + 1 < B:
                    q_diag(n // U + 1)
                if n == 7:
                    row = 0
                    for routed, shared in ((b1, sb1), (b3, sb3), (b2, sb2)):
                        for src in (routed.rearrange("e (r p) -> (e r) p", p=P), shared.rearrange("(r p) -> r p", p=P)):
                            sp.dma_start(bias_f[row:row + src.shape[0], :], src).then_inc(s_biasf, 16)
                            row += src.shape[0]
                    sp.wait_ge(c_pool, 4)
                    sp.dma_start(xs.ap()[DUMMY:DUMMY + P, :], pad_row[:]).then_inc(s_dummy, 16)
                if n >= 11 and n % 4 == 3 and (n - 11) // 4 <= E:
                    expert_weights((n - 11) // 4)
                if n == 30:
                    sp.wait_ge(bias_step, 5)
                    sp.dma_start(bias_scr.ap().rearrange("t r n -> r t n"), bparts[:]).then_inc(s_biasw, 16)
                if n == 34:
                    sp.wait_ge(s_biasw, 16)
                    sp.wait_ge(c_bias, 1)
                    row = 0
                    for k, rows in enumerate(BROWS):
                        sp.dma_start(bias3[3 * k:3 * k + 3, 0:rows * P],
                                     bias_scr.ap()[:, row:row + rows, :].rearrange("t r n -> t (r n)")).then_inc(s_bias3, 16)
                        row += rows
            sp.wait_ge(pad_sb, 1)
            for e in range(E):
                row = sp.value_load(pad_start[0:1, e:e + 1], min_val=0, max_val=DUMMY - P)
                sp.dma_start(xs.ap()[bass.ds(row, P), :], pad_row[:]).then_inc(s_pad, 16)
            sp.wait_ge(s_scat, 16 * 2 * B)
            sp.wait_ge(s_pad, 16 * E)
            sp.wait_ge(s_dummy, 16)
            sp.wait_ge(tab_sb, 1)
            for r in range(5):
                load(r, r % 2)
            with sp.Fori(0, (NR - 5) // 2) as q:
                for u in range(2):
                    load(q * 2 + (5 + u), 1 - u)
            for r in range(5 + 2 * ((NR - 5) // 2), NR):
                load(r, r % 2)
            for par in range(2):
                sp.wait_ge(s_ysc[par], 16 * ((NR - 1 - par) // 2 + 1))
            for g in range(NG):
                for k in range(2):
                    sp.dma_start(Y[k][:, g * G4:(g + 1) * G4, :],
                                 ys.ap()[k * TOKENS + g * G4 * P:k * TOKENS + (g + 1) * G4 * P, :].rearrange(
                                     "(b s) d -> s b d", s=P)).then_inc(s_y[g], 16)
            for g in range(NG):
                sp.wait_ge(fo_sb, g + 1)
                if g == NG - 1:
                    sp.wait_ge(fo2_sb, 1)
                sp.dma_start(out[g * G4:(g + 1) * G4].rearrange("b s d -> s b d"), Z[:, g * G4:(g + 1) * G4, :]).then_inc(s_out, 16)
            sp.wait_ge(s_out, 16 * NG)

        @block.gpsimd
        def _(pool):
            pool.memset(ident[:], 0.0).then_inc(c_ident, 1)
            pool.memset(ones[:], 1.0)
            pool.memset(pad_row[:], 0.0).then_inc(c_zero, 1)
            pool.wait_ge(c_ident, 1)
            pool.affine_select(out=ident[:], in_=ident[:], compare_op=ALU.not_equal, fill=1.0, base=0,
                               pattern=[[-1, P]], channel_multiplier=1).then_inc(c_ident, 1)
            pool.memset(Kst[:].bitcast(F32), 1.0)
            pool.memset(Qst[:].bitcast(F32), 0.0).then_inc(c_pool, 1)
            pool.memset(Qdiag[:].bitcast(F32), 0.0).then_inc(c_pool, 1)
            pool.memset(head_ones[:], 0.0).then_inc(c_pool, 1)
            pool.memset(neg_half[:], -0.5)
            pool.memset(zero[:], 0.0)
            pool.memset(bias3[:], 0.0).then_inc(c_bias, 1)
            pool.memset(bias_rows[:], 1.0).then_inc(c_bias, 1)
            pool.wait_ge(c_bias, 2)
            pool.affine_select(out=bias_rows[:], in_=bias_rows[:], compare_op=ALU.is_ge, fill=0.0, base=0,
                               pattern=[[-3, 3], [0, P]], channel_multiplier=1).then_inc(c_bias, 1)
            pool.wait_ge(c_bias, 3)
            pool.affine_select(out=bias_rows[:], in_=bias_rows[:], compare_op=ALU.is_ge, fill=0.0, base=2,
                               pattern=[[3, 3], [0, P]], channel_multiplier=-1).then_inc(c_bias, 1)
            pool.wait_ge(c_pool, 3)
            for j in range(U):
                pool.memset(head_ones[:, j, HD * j:HD * (j + 1)], 1.0)
            pool.wait_ge(c_zero, 1)
            pool.affine_select(out=before[:], in_=ones[:], compare_op=ALU.is_gt, fill=0.0, base=0,
                               pattern=[[1, P]], channel_multiplier=-1)
            pool.iota(iota8[:], [[1, E]], base=-E, channel_multiplier=0, allow_small_or_imprecise_dtypes=True)
            pool.iota(iota_t[:], [[1, NR]], base=0, channel_multiplier=0, allow_small_or_imprecise_dtypes=True)
            pool.iota(iota_rows[:], [[P, NR]], base=0, channel_multiplier=0, allow_small_or_imprecise_dtypes=True)
            pool.iota(region[:], [[CAP, E]], base=0, channel_multiplier=0, allow_small_or_imprecise_dtypes=True)
            pool.iota(dest[:], [[TOKENS, 2], [P, B]], base=0, channel_multiplier=1, allow_small_or_imprecise_dtypes=True)
            pool.iota(pad_row[:, D:D + 1], [[0, 1]], base=2 * TOKENS, channel_multiplier=1, allow_small_or_imprecise_dtypes=True)
            pool.memset(expert_of[:], E).then_inc(c_pool, 1)

            def root(ag, ve, rs, mv, out_ve, out_rs, b):
                p = b % 2
                pool.wait_ge(ag, b + 1)
                pool.tensor_scalar(out_ve[:, p:p + 1], mv[:, p, 1:2], EPS, None, ALU.add).then_inc(ve, 1)
                pool.wait_ge(ve, b + 1)
                pool.tensor_tensor(out_rs[:, p:p + 1], out_ve[:, p:p + 1], neg_half[:], ALU.pow).then_inc(rs, 1)

            def mark(g, k):
                if k == 0:
                    pool.wait_ge(slots_sb, g + 1)
                    pool.wait_ge(x2_sb, G4 * (g + 1))
                else:
                    pool.wait_ge(s_scat, 16 * G4 * (2 * g + 1))
                rows = X2[:, g * G4:(g + 1) * G4, :]
                pool.tensor_copy(rows[:, :, D:D + 1].rearrange("p b o -> p (b o)"), dest[:, k, g * G4:(g + 1) * G4])
                pool.tensor_copy(rows[:, :, D + 1:D + 2].rearrange("p b o -> p (b o)"),
                                 weight[:, k, g * G4:(g + 1) * G4]).then_inc(marked, 1)
                pool.wait_ge(marked, 2 * g + k + 1)

            def scatter(g, i):
                k, b = i // G4, g * G4 + i % G4
                if i % G4 == 0:
                    mark(g, k)
                pool.indirect_dma_start(xs.ap(), bass.IndirectOffsetOnAxis(ap=slot[:, k, b:b + 1], axis=0),
                                        X2[:, b, :], None).then_inc(s_scat, 16)

            for n in range(FIRST_SLOT, LAST_SLOT + 1):
                for b, k in chain_steps(n):
                    p = b % 2
                    if k == 1:
                        root(mv_sb, ve_sb, rs_sb, meanvar, vareps, rstd, b)
                    elif k == 2:
                        pool.wait_ge(x1_sb, b + 1)
                        pool.tensor_tensor(X1B[:, p, :], X1[:, p, :], bqv_row[:], ALU.add).then_inc(x1b_sb, 1)
                    elif k == 5:
                        pool.wait_ge(hq_sb, b + 1)
                        pool.tensor_tensor(hq_x[:, p, :], X1T[:, p, :], hqT[:, p, :], ALU.mult).then_inc(hqx_sb, 1)
                    elif k == 7:
                        root(mv2_sb, ve2_sb, rs2_sb, meanvar2, vareps2, rstd2, b)
                for g in range(NG - 1):
                    if 0 <= n - (G4 * U * g + SCATTER_SLOT) < 2 * G4:
                        scatter(g, n - (G4 * U * g + SCATTER_SLOT))
                if n % U == 0 and 0 <= n // U < B:
                    b = n // U
                    if b == 0:
                        pool.wait_ge(s_small, 16 * SMALL)
                    if b % G4 == 0:
                        pool.wait_ge(s_x[b // G4], 16)
                    if b >= 2:
                        pool.wait_ge(r_sb, b - 1)
                    pool.tensor_tensor(XB[:, b % 2, :], X[:, b, :], bo_row[:], ALU.add).then_inc(xb_sb, 1)
                if n >= 14 and n % 4 == 2 and (n - 14) // 4 <= E:
                    e = (n - 14) // 4
                    pool.wait_ge(s_w[e], 48)
                    pool.tensor_scalar(W2[:, e * I:(e + 1) * I], W2[:, e * I:(e + 1) * I], 0.5, None, ALU.mult).then_inc(w2_half, 1)
                if n == 10:
                    pool.wait_ge(s_biasf, 96)
                    pool.tensor_copy(bparts[:, 0, :], bias_f[:]).then_inc(bias_step, 1)
                    for part in (1, 2):
                        pool.wait_ge(bias_step, 2 * part - 1)
                        pool.tensor_tensor(bias_f[:], bias_f[:], bparts[:, part - 1, :], ALU.subtract).then_inc(bias_step, 1)
                        pool.wait_ge(bias_step, 2 * part)
                        pool.tensor_copy(bparts[:, part, :], bias_f[:]).then_inc(bias_step, 1)
            for i in range(LAST_SLOT + 1 - (G4 * U * (NG - 2) + SCATTER_SLOT), 2 * G4):
                scatter(NG - 2, i)
            for i in range(2 * G4):
                scatter(NG - 1, i)

            def add_shared(g):
                pos = G4 * (g + 1) - 1
                pool.wait_ge(y_sb, (pos if pos < NA else NR + pos) + 1)
                pool.tensor_tensor(Z[:, g * G4:(g + 1) * G4, :], Z[:, g * G4:(g + 1) * G4, :], X2[:, g * G4:(g + 1) * G4, 0:D],
                                   ALU.add).then_inc(f1_sb, 1)

            for g in range((NA - 2) // G4):
                add_shared(g)

            def meta(ring, loads, placed):
                pool.wait_ge(s_load[ring % 2], 16 * loads)
                if placed is not None:
                    pool.wait_ge(s_ysc[ring % 2], 16 * placed)
                pool.tensor_tensor(row_weight[:, ring:ring + 1], XR[:, ring % 2, D + 1:D + 2], zero[:], ALU.add)
                pool.tensor_copy(row_dest[:, ring:ring + 1], XR[:, ring % 2, D:D + 1]).then_inc(meta_sb, 1)

            def place(i, ring, loads, placed):
                pool.wait_ge(y_sb, NA + 1 + i)
                if loads is not None:
                    meta((ring + 3) % 4, loads, placed)
                else:
                    pool.wait_ge(s_ysc[1 - ring % 2], 16 * placed)
                pool.wait_ge(meta_sb, 3)
                pool.indirect_dma_start(ys.ap(), bass.IndirectOffsetOnAxis(ap=row_dest[:, ring:ring + 1], axis=0),
                                        YO[:, ring % 2, :], None).then_inc(s_ysc[ring % 2], 16)

            def place_static(i):
                place(i, i % 4, (i + 3) // 2 + 1 if i + 3 < NR else None, (i - 1) // 2 + 1 if i else None)

            for i in range(3):
                meta(i, i // 2 + 1, None)
            for i in range(4):
                place_static(i)
            with pool.Fori(0, QUADS) as q:
                for u in range(4):
                    place(q * 4 + (4 + u), u, q * 2 + ((7 + u) // 2 + 1), q * 2 + ((3 + u) // 2 + 1))
            for i in range(4 + 4 * QUADS, NR):
                place_static(i)
            for g in range((NA - 2) // G4, NG):
                add_shared(g)
            for g in range(NG):
                here = slice(g * G4, (g + 1) * G4)
                mean, var = (meanvar3[:, here, i:i + 1].rearrange("p b o -> p (b o)") for i in range(2))
                pool.wait_ge(fm_sb, G4 * (g + 1))
                pool.tensor_scalar(vareps3[:, here], var, EPS, None, ALU.add).then_inc(fv_sb, 1)
                pool.tensor_scalar(shift3[:, here], mean, -1.0, None, ALU.mult).then_inc(fv_sb, 1)
                pool.wait_ge(fv_sb, 2 * g + 1)
                pool.tensor_tensor(rstd3[:, here], vareps3[:, here], neg_half[:].to_broadcast([P, G4]), ALU.pow).then_inc(fr_sb, 1)
                pool.wait_ge(fr_sb, 2 * g + 1)
                pool.wait_ge(fv_sb, 2 * g + 2)
                pool.tensor_tensor(shift3[:, here], shift3[:, here], rstd3[:, here], ALU.mult).then_inc(fr_sb, 1)

        @block.scalar
        def _(act):
            def context(q):
                act.wait_ge(cT_ps, q + 1)
                act.wait_ge(sr_sb, q + 1)
                act.copy(ctxT[:], pX[:, 1, 0:4 * NC]).then_inc(cT_sb, 1)
                act.wait_ge(row_ps, q + 1)
                act.activation(sim_row[32 * q:32 * q + 1, :], pX[32 * q:32 * q + 1, 0, 0:4 * NC], ACT.Identity,
                               bias=bsim[32 * q:32 * q + 1, :], scale=1.0).then_inc(row_sb, 1)

            def group(g, k):
                if k == 0:
                    act.wait_ge(xT_ps, g + 1)
                    if g >= 2:
                        act.wait_ge(v_ps, G4 * (g - 1))
                    act.copy(XT[:, g % 2, :], pM[:]).then_inc(xT_sb, 1)
                else:
                    i = k - 1
                    if g == 0 and k == 1:
                        act.wait_ge(s_qkb, 32)
                    act.wait_ge(qk_ps, 2 * g + i + 1)
                    if g:
                        act.wait_ge(s_parts[i][g - 1], 48)
                    act.activation(qk_hi[:, i, :], pM[:], ACT.Identity, bias=qk_bias[:, i:i + 1],
                                   scale=1.0).then_inc(hi_sb, 1)

            def exps(u):
                act.wait_ge(sT_ps, u + 1)
                if u >= 4:
                    act.wait_ge(pv_ps, u - 3)
                act.activation(PT[:, u % 4, :], pT[:, u % 2, :], ACT.Exp, scale=SCALE).then_inc(p_sb, 1)

            def chain(b, k):
                p = b % 2
                if k == 2:
                    act.wait_ge(x1T_ps, b + 1)
                    act.copy(X1T[:, p, :], pX[:, p, 0:P]).then_inc(x1T_sb, 1)
                elif k == 3:
                    act.wait_ge(nm_sb, b + 1)
                    act.activation(Aexp[:, p, :], pX[:, p, 0:NC], ACT.Exp, bias=neg_rowmax[:, p:p + 1], scale=1.0,
                                   accum_out=Asum[:, p:p + 1]).then_inc(ae_sb, 1)
                elif k == 4:
                    act.wait_ge(top_sb, b + 1)
                    act.activation(batt[:, p, :], pX[0:1, p, P:2 * P], ACT.Exp, bias=top[:, p:p + 1], scale=-1.0,
                                   accum_out=batt_sum[:, p:p + 1]).then_inc(be_sb, 1)
                    act.copy(AT[:, p, :], pX[0:NC, p, 0:P]).then_inc(aT_sb, 1)
                elif k == 5:
                    act.wait_ge(hq_ps, b + 1)
                    act.copy(batt_col[:, p:p + 1], pX[:, p, P:P + 1])
                    act.copy(hqT[:, p, :], pX[:, p, 0:P]).then_inc(hq_sb, 1)
                elif k == 6:
                    act.wait_ge(hc_ps, b + 1)
                    act.copy(hc[:, p:p + 1], pX[:, p, 0:1]).then_inc(hc_sb, 1)
                elif k == 8:
                    act.wait_ge(x2T_ps, b + 1)
                    act.copy(X2T[:, p, :], pX[:, p, 0:P]).then_inc(x2T_sb, 1)

            def copy_logits(b):
                act.wait_ge(lg_ps, b + 1)
                act.copy(logit[:, b, :], logit_bank(b)).then_inc(lg_sb, 1)

            def front(n):
                early = [c for c in chain_steps(n) if c[1] in EARLY]
                late = [c for c in chain_steps(n) if c[1] not in EARLY]
                if n >= -2 and n % U == 2 and (n + 2) // U < B:
                    b = (n + 2) // U
                    act.wait_ge(mxT_ps, b + 1)
                    if b >= 2:
                        act.wait_ge(s_maxrow[b % 2], 2 * 16 * (b // 2))
                    act.copy(maxT[:, b % 2, :], pM[0:2 * H, 0:P]).then_inc(mxT_sb, 1)
                for b, k in early:
                    chain(b, k)
                if 0 <= n < U * B:
                    exps(n)
                for b, k in late:
                    chain(b, k)
                if n % U == 1 and 0 <= (n - 13) // U < B:
                    copy_logits((n - 13) // U)
                if group_step(n):
                    group(*group_step(n))

            def tile(m, p, ring, stored, first=False, tanh=True, up=True, y=True):
                act.wait_ge(t_ps, m + 2)
                if first:
                    act.copy(XH[:, p, 2 * P:3 * P], pO[:, 2 * P:3 * P]).then_inc(xh_sb, 1)
                else:
                    act.copy(XH[:, p, :], pO[:, 0:3 * P]).then_inc(xh_sb, 1)
                if tanh:
                    act.wait_ge(g_sb, m)
                    act.activation(th[:, 1 - p, :], gclip[:, 1 - p, :], ACT.Tanh, scale=ALPHA / 2).then_inc(th_sb, 1)
                if up:
                    act.wait_ge(a_ps, m + 1)
                    act.copy(up1[:, p, :], pS[:, p, :]).then_inc(up1_sb, 1)
                if y:
                    act.wait_ge(y_ps, m - 1)
                    if ring is None:
                        act.copy(Z[:, shared_batch(m - 2), :], pM[:, 0:D]).then_inc(y_sb, 1)
                    else:
                        act.wait_ge(meta_sb, m - 1 - NA)
                        if stored is not None:
                            act.wait_ge(s_ysc[p], 16 * stored)
                        act.mul(YO[:, p, :], pM[:, 0:D], row_weight[:, ring:ring + 1]).then_inc(y_sb, 1)

            def tile_static(m):
                i = m - 2 - NA
                routed = 0 <= i < NR
                tile(m, m % 2, i % 4 if routed else None, i // 2 if routed and i >= 2 else None, first=m < 2, tanh=1 <= m <= NT,
                     up=0 <= m < NT, y=m >= 2)

            def route_exp(g):
                act.wait_ge(rlog_sb, g + 1)
                act.activation(rexp[:], logit[:, g * G4:(g + 1) * G4, :], ACT.Exp).then_inc(rexp_sb, 1)

            act.wait_ge(c_ident, 2)
            act.copy(ident_r[:], ident[:]).then_inc(c_identr, 1)
            for n in range(FIRST_SLOT, LAST_SLOT + 1):
                if n == PREP_SLOT:
                    act.wait_ge(gwT_ps, 1)
                    act.copy(gwT[:], pX[:, 0, 0:E]).then_inc(gwT_sb, 1)
                    for q in range(4):
                        context(q)
                front(n)
                for g in range(NG - 1):
                    if n == G4 * U * g + ROUTE_SLOT:
                        route_exp(g)
                if n >= FFN_SLOT - 1:
                    tile_static(n - FFN_SLOT)
            copy_logits(B - 1)
            for m in range(LAST_SLOT - FFN_SLOT + 1, LOOP):
                if m == ROUTE:
                    route_exp(NG - 1)
                tile_static(m)
            with act.Fori(0, QUADS) as q:
                for u in range(4):
                    tile(q * 4 + (LOOP + u), u % 2, (2 + u) % 4, q * 2 + (1 + u // 2))
            for m in range(LOOP + 4 * QUADS, NT + 2):
                tile_static(m)
            for g in range(NG):
                act.wait_ge(fr_sb, 2 * (g + 1))
                for b in range(g * G4, min((g + 1) * G4, B - 2)):
                    ins = act.activation(Z[:, b, :], S[:, g, (b % G4) * D:(b % G4 + 1) * D], ACT.Identity, bias=shift3[:, b:b + 1],
                                         scale=rstd3[:, b:b + 1])
                ins.then_inc(fo_sb, 1)

        @block.vector
        def _(dve):
            def context(q):
                dve.wait_ge(cT_ps, q + 1)
                dve.tensor_scalar(sim_rhs[:, 4 * q:4 * q + 4, :], pX[:, 1, 0:4 * NC].rearrange("p (b j) -> p b j", b=4),
                                  wsim[:, 2:3], wsim[:, 0:1], ALU.mult, ALU.add).then_inc(sr_sb, 1)

            def group(g, k):
                if k:
                    i = k - 1
                    dve.wait_ge(hi_sb, 2 * g + i + 1)
                    dve.scalar_tensor_tensor(out=qk_lo[:, i, :], in0=pM[:], scalar=qk_bias[:, i:i + 1],
                                             in1=qk_hi[:, i, :].bitcast(F32), op0=ALU.add, op1=ALU.subtract).then_inc(lo_sb, 1)

            def values(b):
                dve.wait_ge(v_ps, b + 1)
                if b == 0:
                    dve.wait_ge(c_v, 1)
                if b >= 2:
                    dve.wait_ge(pv_ps, U * (b - 1))
                to = bass.AP(Vz, (b % 2) * HG * U * 32, [[2 * HG * U * 32, P], [U * 32, HG], [32 + HD, U], [1, HD]])
                dve.tensor_tensor(to, pM[:, 0:D].rearrange("p (g j d) -> p g j d", g=HG, j=U),
                                  bv_row[:].rearrange("p (g j d) -> p g j d", g=HG, j=U), ALU.add).then_inc(v_sb, 1)

            def row_max(u):
                b, j = u // U, u % U
                dve.wait_ge(s_ps, u + 1)
                dve.tensor_reduce(out=negmax[:, b % 2, HG * j:HG * (j + 1)],
                                  in_=pS[:, u % 2, :].rearrange("p (g k) -> p g k", g=HG), axis=AX.X, op=ALU.max,
                                  negate=True).then_inc(max_sb, 1)
                if j == U - 1:
                    dve.wait_ge(max_sb, u + 1)
                    if b >= 1:
                        dve.wait_ge(mxT_ps, b)
                    dve.tensor_copy(max_parts[:, 0, :], negmax[:, b % 2, :]).then_inc(mx_hi, 1)
                    dve.wait_ge(mx_hi, b + 1)
                    dve.tensor_tensor(max_parts[:, 1, :], negmax[:, b % 2, :], max_parts[:, 0, :].bitcast(F32),
                                      ALU.subtract).then_inc(mx_parts, 1)

            def denominators(b):
                dve.wait_ge(pv_ps, U * (b + 1))
                dve.reciprocal(inv_den[:, b % 2, :], pO[:, P:2 * P]).then_inc(inv_sb, 1)

            def attention_out(b):
                p = b % 2
                dve.wait_ge(inv_sb, b + 1)
                dve.tensor_tensor(attnT[:, p, :], pO[:, 0:P], inv_den[:, p, :], ALU.mult).then_inc(attn_sb, 1)

            def norm_stats(b, src, st, mv, s_src, s_st, s_mv):
                p = b % 2
                dve.wait_ge(s_src, b + 1)
                dve.bn_stats(st[:, p, :], src[:, p, :]).then_inc(s_st, 1)
                dve.wait_ge(s_st, b + 1)
                dve.bn_aggr(mv[:, p, :], st[:, p, :]).then_inc(s_mv, 1)

            def chain_a(b, k):
                p = b % 2
                if k == 1:
                    dve.wait_ge(o_ps, b + 1)
                    dve.wait_ge(xb_sb, b + 1)
                    dve.tensor_tensor(R[:, p, :], pX[:, p, 0:D], XB[:, p, :], ALU.add).then_inc(r_sb, 1)
                    norm_stats(b, R, stats, meanvar, r_sb, st_sb, mv_sb)
                elif k == 3:
                    dve.wait_ge(sim_ps, b + 1)
                    dve.tensor_reduce(out=neg_rowmax[:, p:p + 1], in_=pX[:, p, 0:NC], axis=AX.X, op=ALU.max,
                                      negate=True).then_inc(nm_sb, 1)
                elif k == 4:
                    dve.wait_ge(aT_ps, b + 1)
                    dve.tensor_reduce(out=top[:, p:p + 1], in_=pX[0:1, p, P:2 * P], axis=AX.X, op=ALU.min).then_inc(top_sb, 1)
                elif k == 6:
                    dve.wait_ge(hc_sb, b + 1)
                    dve.scalar_tensor_tensor(out=wx[:, p, :], in0=wqv[:, 3, :], scalar=hc[:, p:p + 1], in1=wqv[:, 0, :],
                                             op0=ALU.mult, op1=ALU.add).then_inc(wx_sb, 1)
                elif k == 7:
                    dve.wait_ge(x2_ps, b + 1)
                    dve.wait_ge(x1b_sb, b + 1)
                    dve.tensor_tensor(R2[:, p, :], pX[:, p, 0:D], X1B[:, p, :], ALU.add).then_inc(r2_sb, 1)
                    norm_stats(b, R2, stats2, meanvar2, r2_sb, st2_sb, mv2_sb)

            def chain_b(b, k):
                p = b % 2
                if k == 1:
                    dve.wait_ge(rs_sb, b + 1)
                    dve.tensor_scalar(X1[:, p, :], R[:, p, :], meanvar[:, p, 0:1], rstd[:, p:p + 1], ALU.subtract,
                                      ALU.mult).then_inc(x1_sb, 1)
                elif k == 3:
                    dve.wait_ge(ae_sb, b + 1)
                    dve.reciprocal(Ainv[:, p:p + 1], Asum[:, p:p + 1]).then_inc(ai_sb, 1)
                    dve.wait_ge(ai_sb, b + 1)
                    dve.tensor_scalar(A[:, p, :], Aexp[:, p, :], Ainv[:, p:p + 1], None, ALU.mult).then_inc(a_sb, 1)
                elif k == 7:
                    dve.wait_ge(rs2_sb, b + 1)
                    dve.tensor_scalar(X2[:, b, 0:D], R2[:, p, :], meanvar2[:, p, 0:1], rstd2[:, p:p + 1], ALU.subtract,
                                      ALU.mult).then_inc(x2_sb, 1)

            def front(n):
                steps = chain_steps(n)
                for b, k in chain_steps(n - 1):
                    chain_b(b, k)
                for b, k in steps:
                    if k in EARLY:
                        chain_a(b, k)
                if 0 <= n + LEAD < U * B:
                    row_max(n + LEAD)
                for b, k in steps:
                    if k not in EARLY:
                        chain_a(b, k)
                if n % U == 0 and 1 <= n // U <= B:
                    denominators(n // U - 1)
                for b, k in steps:
                    if k == 4:
                        dve.wait_ge(be_sb, b + 1)
                        dve.reciprocal(batt_inv[:, b % 2:b % 2 + 1], batt_sum[:, b % 2:b % 2 + 1]).then_inc(bi_sb, 1)
                if n % U == 0 and 1 <= n // U <= B:
                    attention_out(n // U - 1)
                if group_step(n):
                    group(*group_step(n))
                if n % U == U - 1 and 0 <= (n + 1) // U < B:
                    values((n + 1) // U)

            def tile(i, p):
                dve.wait_ge(b_ps, i + 1)
                dve.wait_ge(up1_sb, i + 1)
                dve.tensor_tensor(prod[:, p, :], pT[:, p, :], up1[:, p, :], ALU.mult).then_inc(prod_sb, 1)
                dve.wait_ge(prod_sb, i + 1)
                dve.tensor_scalar(gclip[:, p, :], prod[:, p, 0:I2:2], LIMIT, None, ALU.min).then_inc(g_sb, 1)
                dve.tensor_scalar(lclip[:, p, :], prod[:, p, 1:I2:2], LIMIT, -LIMIT, ALU.min, ALU.max).then_inc(l_sb, 1)
                dve.wait_ge(th_sb, i + 1)
                dve.scalar_tensor_tensor(out=gate[:, p, :], in0=th[:, p, :], scalar=1.0, in1=gclip[:, p, :], op0=ALU.add,
                                         op1=ALU.mult).then_inc(gt_sb, 1)
                dve.wait_ge(l_sb, i + 1)
                dve.wait_ge(gt_sb, i + 1)
                dve.scalar_tensor_tensor(out=hid[:, p, :], in0=lclip[:, p, :], scalar=1.0, in1=gate[:, p, :], op0=ALU.add,
                                         op1=ALU.mult).then_inc(h_sb, 1)

            steps_done = [0]

            def link(ins):
                steps_done[0] += 1
                ins.then_inc(rt, 1)
                dve.wait_ge(rt, steps_done[0])

            def over_e(t):
                return t[:].rearrange("p (b o) -> p b o", o=1).to_broadcast([P, G4, E])

            def of_e(t):
                return bass.AP(t, 0, [[E, P], [0, G4], [1, E]])

            def over_k(t):
                return bass.AP(t, 0, [[G4 * E, P], [0, 2], [E, G4], [1, E]])

            def largest(g):
                dve.wait_ge(lg_sb, G4 * (g + 1))
                if g:
                    dve.wait_ge(rexp_sb, g)
                here = logit[:, g * G4:(g + 1) * G4, :]
                link(dve.tensor_reduce(out=rtop[:], in_=here, axis=AX.X, op=ALU.max))
                dve.tensor_tensor(here, here, over_e(rtop), ALU.subtract).then_inc(rlog_sb, 1)

            def choose_a(src):
                link(dve.tensor_reduce(out=rtop[:], in_=src[:], axis=AX.X, op=ALU.max))
                link(dve.tensor_tensor(cand[:], src[:], over_e(rtop), ALU.is_ge))
                link(dve.tensor_tensor(cand[:], cand[:], of_e(iota8), ALU.mult))

            def choose_b(k):
                link(dve.tensor_reduce(out=rtop[:], in_=cand[:], axis=AX.X, op=ALU.min))
                link(dve.tensor_tensor(pick[:, k], of_e(iota8), over_e(rtop), ALU.is_equal))

            def softmax_and_bias(g):
                dve.wait_ge(rexp_sb, g + 1)
                link(dve.tensor_reduce(out=rtop[:], in_=rexp[:], axis=AX.X, op=ALU.add))
                link(dve.reciprocal(rinv[:], rtop[:]))
                link(dve.tensor_tensor(biased[:], rexp[:], over_e(rinv), ALU.mult))
                link(dve.tensor_tensor(biased[:], biased[:], of_e(gateb_row), ALU.add))

            def weights(g):
                link(dve.tensor_tensor(picked_of[:], pick[:], over_k(rexp), ALU.mult))
                link(dve.tensor_reduce(out=weight_f[:], in_=picked_of[:], axis=AX.X, op=ALU.add))
                link(dve.tensor_tensor(weight[:, :, g * G4:(g + 1) * G4], weight_f[:], bass.AP(rinv, 0, [[G4, P], [0, 2], [1, G4]]),
                                       ALU.mult))

            def first_rows(g):
                bank = count_bank(g).rearrange("p (k b e) -> p k b e", k=2, b=G4)
                link(dve.tensor_copy(first_row[:, 0, :], region[:] if g == 0 else first_row[:, G4, :]))
                dve.wait_ge(cnt_ps, g + 1)
                for c in range(G4):
                    link(dve.tensor_tensor(first_row[:, c + 1, :], first_row[:, c, :], bank[:, 1, c, :], ALU.add))
                dve.tensor_tensor(cand[:], bank[:, 0], first_row[:, 0:G4, :], ALU.add).then_inc(cnt_sb, 1)

            def choice_rows(g):
                dve.wait_ge(cnt_sb, g + 1)
                link(dve.tensor_tensor(picked_of[:], pick[:], over_k(cand), ALU.mult))
                link(dve.tensor_reduce(out=slot_f[:], in_=picked_of[:], axis=AX.X, op=ALU.add))
                dve.tensor_copy(slot[:, :, g * G4:(g + 1) * G4], slot_f[:]).then_inc(slots_sb, 1)

            def padding_rows():
                dve.tensor_copy(pad_start[:], first_row[0:1, G4, :]).then_inc(pad_sb, 1)

            def expert_tiles():
                link(dve.tensor_tensor(total[:], first_row[:, G4, :], region[:], ALU.subtract))
                link(dve.tensor_scalar(tiles[:], total[:], 1.0 / P, (P - 1) / (2.0 * P), ALU.mult, ALU.add))
                link(dve.tensor_scalar(tiles[:], tiles[:], float(1 << 23), None, ALU.add))
                link(dve.tensor_scalar(tiles[:], tiles[:], float(1 << 23), None, ALU.subtract))
                link(dve.tensor_tensor_scan(tiles_cum[:], ones[:, 0:E], tiles[:], 0.0, ALU.mult, ALU.add))
                link(dve.tensor_tensor(total[:], tiles_cum[:], tiles[:], ALU.subtract))
                link(dve.memset(start[:, E:E + 1], float(DUMMY)))
                link(dve.scalar_tensor_tensor(out=start[:, 0:E], in0=total[:], scalar=float(-P), in1=region[:], op0=ALU.mult, op1=ALU.add))
                link(dve.tensor_tensor(step[:], start[:, 1:E + 1], start[:, 0:E], ALU.subtract))

            def tile_table():
                link(dve.tensor_tensor(past[:], iota_t[:].rearrange("p (t o) -> p t o", o=1).to_broadcast([1, NR, E]),
                                       bass.AP(tiles_cum, 0, [[E, 1], [0, NR], [1, E]]), ALU.is_ge))
                link(dve.tensor_reduce(out=tab_f[:], in_=past[:], axis=AX.X, op=ALU.add))
                link(dve.tensor_scalar(expert_of[:, NA:NA + NR], tab_f[:], float(E - 1), None, ALU.min))
                link(dve.tensor_tensor(past_step[:], past[:], bass.AP(step, 0, [[E, 1], [0, NR], [1, E]]), ALU.mult))
                link(dve.tensor_reduce(out=row_f[:], in_=past_step[:], axis=AX.X, op=ALU.add))
                link(dve.tensor_tensor(row_f[:], row_f[:], iota_rows[:], ALU.add))
                dve.tensor_scalar(row_of[:], row_f[:], float(DUMMY), None, ALU.min).then_inc(tab_sb, 1)

            def routing(g, k):
                if k == 0:
                    largest(g)
                elif k == 1:
                    softmax_and_bias(g)
                elif k == 2:
                    choose_a(biased)
                elif k == 3:
                    choose_b(0)
                    link(dve.scalar_tensor_tensor(out=biased[:], in0=pick[:, 0], scalar=-BIG, in1=biased[:], op0=ALU.mult,
                                                  op1=ALU.add))
                elif k == 4:
                    choose_a(biased)
                elif k == 5:
                    choose_b(1)
                    dve.tensor_tensor(both[:], pick[:, 0], pick[:, 1], ALU.add).then_inc(picked, 1)
                elif k == 6:
                    weights(g)
                elif k == COUNT_STEP:
                    first_rows(g)
                elif k == COUNT_STEP + 1:
                    choice_rows(g)

            def sum_choices(g):
                here = slice(g * G4, (g + 1) * G4)
                dve.wait_ge(s_y[g], 32)
                dve.tensor_tensor(S[:, g, :].rearrange("p (b d) -> p b d", b=G4), Y[0][:, here, :], Y[1][:, here, :],
                                  ALU.add).then_inc(f2_sb, 1)

            def final_sums(g):
                here = slice(g * G4, (g + 1) * G4)
                sums = S[:, g, :].rearrange("p (b d) -> p b d", b=G4)
                dve.wait_ge(f2_sb, g + 1)
                dve.wait_ge(f1_sb, g + 1)
                dve.tensor_tensor(sums, sums, Z[:, here, :], ALU.add).then_inc(f3_sb, 1)
                dve.wait_ge(f3_sb, g + 1)
                for c in range(G4):
                    dve.bn_stats(stats3[:, g * G4 + c, :], sums[:, c, :]).then_inc(fs_sb, 1)
                if g + 1 < NG:
                    sum_choices(g + 1)
                for c in range(G4):
                    dve.wait_ge(fs_sb, g * G4 + c + 1)
                    dve.bn_aggr(meanvar3[:, g * G4 + c, :], stats3[:, g * G4 + c, :]).then_inc(fm_sb, 1)

            dve.memset(Kdiag[:].bitcast(F32), 0.0).then_inc(c_kdiag, 1)
            dve.memset(Vz[:], 0.0).then_inc(c_v, 1)
            for n in range(FIRST_SLOT, LAST_SLOT + 1):
                if n == PREP_SLOT:
                    dve.wait_ge(s_small, 16 * SMALL)
                    for q in range(4):
                        context(q)
                front(n)
                for g in range(NG - 1):
                    if n == G4 * U * g + ROUTE_SLOT and g == 0:
                        dve.wait_ge(c_pool, 4)
                    routing(g, n - G4 * U * g - ROUTE_SLOT)
                if n >= FFN_SLOT + 1:
                    tile(n - FFN_SLOT - 1, (n - FFN_SLOT - 1) % 2)
            for m in range(LAST_SLOT - FFN_SLOT + 1, LOOP):
                for k in {ROUTE: range(1), ROUTE + 1: range(1, COUNT_STEP), ROUTE + 2: range(COUNT_STEP, ROUTE_STEPS)}.get(m, ()):
                    routing(NG - 1, k)
                if m == ROUTE + 2:
                    padding_rows()
                if m == ROUTE + 3:
                    expert_tiles()
                if m == ROUTE + 4:
                    tile_table()
                tile(m - 1, (m - 1) % 2)
            with dve.Fori(0, PAIRS) as q:
                for u in range(2):
                    tile(q * 2 + (LOOP - 1 + u), (LOOP - 1 + u) % 2)
            for m in range(LOOP + 2 * PAIRS, NT + 1):
                tile(m - 1, (m - 1) % 2)
            sum_choices(0)
            for g in range(NG):
                final_sums(g)
            dve.wait_ge(fr_sb, 2 * NG)
            for b in range(B - 2, B):
                ins = dve.tensor_scalar(Z[:, b, :], S[:, NG - 1, (b % G4) * D:(b % G4 + 1) * D], rstd3[:, b:b + 1], shift3[:, b:b + 1],
                                        ALU.mult, ALU.add)
            ins.then_inc(fo2_sb, 1)

        @block.tensor
        def _(pe):
            issued = {"qk": 0, "v": 0, "x": 0, "m": 0, "l": 0, "c": 0}

            def projections_free():
                for s, k in ((xT_sb, "x"), (lo_sb, "qk"), (v_sb, "v"), (mxT_sb, "m"), (lg_sb, "l"), (cnt_sb, "c")):
                    if issued[k]:
                        pe.wait_ge(s, issued[k])

            def group(g, k):
                projections_free()
                if k == 0:
                    pe.wait_ge(s_x[g], 16)
                    pe.wait_ge(c_ident, 2)
                    for c in range(G4):
                        mm = pe.transpose(pM[:, c * P:(c + 1) * P], X[:, g * G4 + c, :], ident[:])
                    mm.then_inc(xT_ps, 1)
                    issued["x"] += 1
                else:
                    pe.wait_ge(s_circ, 64)
                    pe.wait_ge(xT_sb, g + 1)
                    pe.matmul(pM[:], circ[:, k - 1, :], XT[:, g % 2, :], start=True, stop=True).then_inc(qk_ps, 1)
                    issued["qk"] += 1

            def values(b):
                projections_free()
                pe.matmul(pM[:, 0:D], XT[:, (b // G4) % 2, qcols(b)], circ[:, 2, :], start=True, stop=True).then_inc(v_ps, 1)
                issued["v"] += 1

            def scores(u):
                b, j = u // U, u % U
                pe.wait_ge(s_qst[(b // 2) % 2], HG * 16 * (b // 4 + 1))
                pe.wait_ge(s_kdiag[b % 2], HG * 16 * (b // 2 + 1))
                if u >= 2:
                    pe.wait_ge(max_sb, u - 1)
                pe.matmul(pS[:, u % 2, :], Qst[:, (b // 2) % 2, j, (b % 2) * P:(b % 2 + 1) * P],
                          Kdiag[:, b % 2, j, :, :], start=True, stop=True).then_inc(s_ps, 1)

            def scores_less_max(u):
                b, j = u // U, u % U
                pe.wait_ge(s_kst[(b // 2) % 2], HG * 16 * (b // 4 + 1))
                pe.wait_ge(s_qdiag[b % 2], HG * 16 * (b // 2 + 1))
                pe.wait_ge(s_maxrow[b % 2], 2 * 16 * (b // 2 + 1))
                if u >= 2:
                    pe.wait_ge(p_sb, u - 1)
                pe.matmul(pT[:, u % 2, :], Kst[:, (b // 2) % 2, j, (b % 2) * P:(b % 2 + 1) * P],
                          Qdiag[:, b % 2, j, :, :], start=True, stop=True).then_inc(sT_ps, 1)

            def weighted_values(u):
                b, j = u // U, u % U
                pe.wait_ge(p_sb, u + 1)
                if u == 0:
                    pe.wait_ge(c_pool, 4)
                if j == 0:
                    pe.wait_ge(v_sb, b + 1)
                    if b >= 1:
                        pe.wait_ge(attn_sb, b)
                for hg in range(HG):
                    pe.matmul(pO[32 * hg:32 * hg + 32, 0:P], Vz[:, b % 2, hg, j, :], PT[:, u % 4, hg * P:(hg + 1) * P],
                              start=(j == 0), stop=(j == U - 1), skip_group_check=True)
                for hg in range(HG):
                    mm = pe.matmul(pO[32 * hg:32 * hg + 32, P:2 * P], head_ones[:, j, :], PT[:, u % 4, hg * P:(hg + 1) * P],
                                   start=False, stop=(j == U - 1), skip_group_check=True)
                mm.then_inc(pv_ps, 1)

            def max_transposes(b):
                projections_free()
                pe.wait_ge(mx_parts, b + 1)
                if b == 0:
                    pe.wait_ge(c_identr, 1)
                pe.matmul(pM[0:2 * H, 0:P], max_parts[:].rearrange("p k h -> p (k h)"), ident_r[:], start=True,
                          stop=True).then_inc(mxT_ps, 1)
                issued["m"] += 1

            def logits(b):
                pe.wait_ge(x2T_sb, b + 1)
                if b < B - 2:
                    projections_free()
                    issued["l"] += 1
                pe.matmul(logit_bank(b), X2T[:, b % 2, :], gwT[:], start=True, stop=True).then_inc(lg_ps, 1)

            def counts(g):
                pe.wait_ge(picked, g + 1)
                if g < NG - 1:
                    projections_free()
                    issued["c"] += 1
                else:
                    pe.wait_ge(lg_sb, B)
                picks = both[:].rearrange("p b e -> p (b e)")
                pe.matmul(count_bank(g)[:, 0:G4 * E], before[:], picks, start=True, stop=True)
                pe.matmul(count_bank(g)[:, G4 * E:2 * G4 * E], ones[:], picks, start=True, stop=True).then_inc(cnt_ps, 1)

            def chain(b, k):
                p = b % 2
                if k == 1:
                    pe.wait_ge(attn_sb, b + 1)
                    if b >= 2:
                        pe.wait_ge(x2T_sb, b - 1)
                    else:
                        pe.wait_ge(row_sb, 4)
                        pe.wait_ge(cT_sb, 4)
                    pe.matmul(pX[:, p, 0:D], attnT[:, p, :], circ[:, 3, :], start=True, stop=True).then_inc(o_ps, 1)
                elif k == 2:
                    pe.wait_ge(x1_sb, b + 1)
                    pe.transpose(pX[:, p, 0:P], X1[:, p, :], ident[:]).then_inc(x1T_ps, 1)
                elif k == 3:
                    pe.wait_ge(x1T_sb, b + 1)
                    pe.wait_ge(sr_sb, 4)
                    pe.matmul(pX[:, p, 0:NC], X1T[:, p, :], sim_rhs[:, b, :], start=True, stop=False)
                    q = 32 * (b // 4)
                    pe.matmul(pX[:, p, 0:NC], ones[q:q + 1, :], sim_row[q:q + 1, (b % 4) * NC:(b % 4 + 1) * NC], start=False,
                              stop=True).then_inc(sim_ps, 1)
                elif k == 4:
                    pe.wait_ge(a_sb, b + 1)
                    pe.transpose(pX[0:NC, p, 0:P], A[:, p, :], ident[:])
                    pe.matmul(pX[0:1, p, P:2 * P], neg_rowmax[:, p:p + 1], ident[:], start=True, stop=True).then_inc(aT_ps, 1)
                elif k == 5:
                    pe.wait_ge(aT_sb, b + 1)
                    pe.wait_ge(s_ctx, 16)
                    pe.matmul(pX[:, p, 0:P], ctx_sb[:, b, :], AT[:, p, :], start=True, stop=True)
                    pe.wait_ge(bi_sb, b + 1)
                    pe.matmul(pX[:, p, P:P + 1], batt[:, p, :], batt_inv[:, p:p + 1], start=True, stop=True).then_inc(hq_ps, 1)
                elif k == 6:
                    pe.wait_ge(hq_sb, b + 1)
                    pe.matmul(pX[:, p, 0:1], X1[:, p, :], batt_col[:, p:p + 1], start=True, stop=True).then_inc(hc_ps, 1)
                elif k == 7:
                    pe.wait_ge(wx_sb, b + 1)
                    pe.wait_ge(hqx_sb, b + 1)
                    pe.matmul(pX[:, p, 0:D], X1T[:, p, :], wx[:, p, :], start=True, stop=False)
                    pe.matmul(pX[:, p, 0:D], hqT[:, p, :], wqv[:, 1, :], start=False, stop=False)
                    pe.matmul(pX[:, p, 0:D], hq_x[:, p, :], wqv[:, 2, :], start=False, stop=True).then_inc(x2_ps, 1)
                elif k == 8:
                    pe.wait_ge(x2_sb, b + 1)
                    pe.transpose(pX[:, p, 0:P], X2[:, b, 0:D], ident[:]).then_inc(x2T_ps, 1)

            def front(n):
                steps = chain_steps(n)
                if 0 <= n + LEAD < U * B:
                    scores(n + LEAD)
                if n >= -2 and n % U == 2 and (n + 2) // U < B:
                    max_transposes((n + 2) // U)
                for b, k in steps:
                    if k in EARLY:
                        chain(b, k)
                if 0 <= n < U * B:
                    scores_less_max(n)
                for b, k in steps:
                    if k in MIDDLE:
                        chain(b, k)
                if 0 <= n - 1 < U * B:
                    weighted_values(n - 1)
                for b, k in steps:
                    if k not in EARLY + MIDDLE:
                        chain(b, k)
                if n % U == 1 and 0 <= (n - 13) // U < B:
                    logits((n - 13) // U)
                if group_step(n):
                    group(*group_step(n))
                if n % U == U - 1 and 0 <= (n + 1) // U < B:
                    values((n + 1) // U)
                for g in range(NG - 1):
                    if n == G4 * U * g + ROUTE_SLOT + COUNT_STEP:
                        counts(g)

            def tile(m, p, rows, loaded, e_up, e_y, hidden=True, up=True, y=True):
                if loaded is not None:
                    pe.wait_ge(s_load[1 - p], 16 * loaded)
                if hidden:
                    pe.wait_ge(h_sb, m - 1)
                pe.wait_ge(xh_sb, m + 1) if not (isinstance(m, int) and m < 0) else None
                if hidden:
                    for k in range(2):
                        mm = pe.transpose(pO[:, k * P:(k + 1) * P], hid[:, p, k * P:(k + 1) * P], ident[:])
                if rows is not None:
                    mm = pe.transpose(pO[:, 2 * P:3 * P], rows, ident[:])
                mm.then_inc(t_ps, 1)

                def product(bank, W, k, done, free):
                    if not (isinstance(m, int) and m < 2):
                        pe.wait_ge(free, m - 1)
                    pe.matmul(bank, XH[:, 1 - p, 2 * P:3 * P], W[:, bass.ds(e_up * I2, I2)], start=True, stop=False)
                    pe.matmul(bank, bias_rows[:, k, :], bias3[:, bass.ds(e_up * I2, I2)], start=False,
                              stop=True).then_inc(done, 1)

                if up:
                    product(pS[:, p, :], W1, 0, a_ps, up1_sb)
                if y:
                    pe.wait_ge(xh_sb, m + 2)
                    if not (isinstance(m, int) and m < 3):
                        pe.wait_ge(y_sb, m - 2)
                    for k in range(2):
                        pe.matmul(pM[:, 0:D], XH[:, p, k * P:(k + 1) * P], W2[:, bass.ds(e_y * I + k * D, D)],
                                  start=(k == 0), stop=False)
                    pe.matmul(pM[:, 0:D], bias_rows[:, 2, :], bias3[:, bass.ds(e_y * D, D)], start=False,
                              stop=True).then_inc(y_ps, 1)
                if up:
                    product(pT[:, p, :], W3, 1, b_ps, prod_sb)

            def expert(i):
                return pe.value_load(expert_of[0:1, bass.ds(i, 1)], min_val=0, max_val=E)

            def tile_static(m, e_up=E, e_y=E):
                rows, loaded = None, None
                if NA <= m + 1 < NA + NR:
                    rows, loaded = XR[:, (m + 1) % 2, 0:D], (m + 1 - NA) // 2 + 1
                elif m + 1 < NT:
                    rows = X2[:, shared_batch(m + 1), 0:D]
                tile(m, m % 2, rows, loaded, e_up, e_y, hidden=m >= 2, up=0 <= m < NT, y=m >= 2)

            for n in range(FIRST_SLOT, LAST_SLOT + 1):
                if n == PREP_SLOT:
                    pe.wait_ge(s_small, 16 * SMALL)
                    pe.transpose(pX[:, 0, 0:E], gw_sb[:], ident[0:E, 0:E]).then_inc(gwT_ps, 1)
                    pe.wait_ge(s_ctx, 16)
                    for q in range(4):
                        if q:
                            pe.wait_ge(cT_sb, q)
                        for c in range(4):
                            mm = pe.transpose(pX[:, 1, c * NC:(c + 1) * NC], ctx_sb[:, 4 * q + c, :], ident[0:NC, 0:NC])
                        mm.then_inc(cT_ps, 1)
                        pe.wait_ge(cT_sb, q + 1)
                        if q:
                            pe.wait_ge(row_sb, q)
                        else:
                            pe.wait_ge(gwT_sb, 1)
                        pe.matmul(pX[32 * q:32 * q + 1, 0, 0:4 * NC], wsim[:, 1:2], ctxT[:], start=True, stop=True).then_inc(row_ps, 1)
                front(n)
                if n == FFN_SLOT - 1:
                    projections_free()
                    pe.wait_ge(attn_sb, B)
                    pe.wait_ge(max_sb, U * B)
                    pe.wait_ge(p_sb, U * B)
                    for e in range(E + 1):
                        pe.wait_ge(s_w[e], 48)
                    pe.wait_ge(w2_half, E + 1)
                    pe.wait_ge(s_bias3, 48)
                    pe.wait_ge(c_bias, 4)
                if n >= FFN_SLOT - 1:
                    tile_static(n - FFN_SLOT)
            logits(B - 1)
            for m in range(LAST_SLOT - FFN_SLOT + 1, LOOP):
                if m == ROUTE + 2:
                    counts(NG - 1)
                if m == NA:
                    pe.wait_ge(tab_sb, 1)
                tile_static(m, e_up=E if m < NA else expert(m), e_y=E if m - 2 < NA else expert(m - 2))
            with pe.Fori(0, PAIRS) as q:
                for u in range(2):
                    m = q * 2 + (LOOP + u)
                    tile(m, u, XR[:, 1 - u, 0:D], q + (5 + u) // 2 + 1, expert(m), expert(m - 2))
            for m in range(LOOP + 2 * PAIRS, NT + 2):
                tile_static(m, e_up=E if m >= NA + NR or m >= NT else expert(m), e_y=E if m - 2 >= NA + NR else expert(m - 2))


_INS = ["x", "ctx_1024", "L0_attn_wq_c", "L0_attn_wq_b", "L0_attn_wk_c", "L0_attn_wk_b", "L0_attn_wv_c", "L0_attn_wv_b",
        "L0_attn_wo_c", "L0_attn_wo_b", "L0_xattn_w_sim", "L0_xattn_b_sim", "L0_xattn_W_qv", "L0_xattn_b_qv",
        "L0_ffn_gate_w", "L0_ffn_gate_b", "L0_ffn_w1", "L0_ffn_b1", "L0_ffn_w3", "L0_ffn_b3", "L0_ffn_w2", "L0_ffn_b2",
        "L0_ffn_sw1", "L0_ffn_sb1", "L0_ffn_sw3", "L0_ffn_sb3", "L0_ffn_sw2", "L0_ffn_sb2"]


def kernel(**inputs):
    import concourse.bacc as _bacc
    from concourse.bass_utils import run_bass_kernel_spmd as _run

    nc = _bacc.Bacc("TRN2", target_bir_lowering=False, num_devices=1)
    arrays, args = {}, []
    for name in _INS:
        a = np.ascontiguousarray(inputs[name])
        arrays[f"in_{name}"] = a
        args.append(nc.dram_tensor(f"in_{name}", a.shape, mybir.dt.from_np(a.dtype), kind="ExternalInput").ap())
    args.append(nc.dram_tensor("out_0", (B, P, D), F32, kind="ExternalOutput").ap())
    decoder_layer(nc, *args)
    r = _run(nc, [arrays], core_ids=[0])
    return r.results[0]["out_0"]
```
